# Optimizing a Trainium2 kernel written in Bass

```python
import numpy as np
import jax
import jax.numpy as jnp

def _softmax(x, axis=-1):
    return jax.nn.softmax(x, axis=axis)

def _gelu(x):
    return jax.nn.gelu(x, approximate=True)

def _silu(x):
    return jax.nn.silu(x)

def _sigmoid(x):
    return jax.nn.sigmoid(x)

def _layernorm(x, axis=-1, eps=1e-05):
    m = jnp.mean(x, axis=axis, keepdims=True)
    v = jnp.var(x, axis=axis, keepdims=True)
    return (x - m) / jnp.sqrt(v + eps)

def _scatter_add(tgt, idx, src, axis=0):
    return tgt.at[idx].add(src)

def _segment_sum(src, seg, n):
    return jax.ops.segment_sum(src, seg, n)
kernel_name = 'mk_adj_resnorm_d4_adj_r2_896148'

def setup_inputs(seed: int=0):
    np.random.seed(seed)
    _w = jnp.asarray

    def _rec_inputs():
        import jax
        import jax.numpy as jnp
        _gk = jax.random.key(seed)
        x = -0.0005963 + 1.001 * jax.random.normal(jax.random.fold_in(_gk, 1), (3327, 256), jnp.float32)
        _a = jax.random.bernoulli(jax.random.fold_in(_gk, 2), 0.00120228, (3327, 3327))
        _af = _a.astype(jnp.float32)
        adj = _af
        return (x, adj)
    x, adj = _rec_inputs()

    def _L0_gnn_setup():
        import jax, jax.numpy as jnp
        import numpy as np
        N = 3072
        D_IN = 256
        D_OUT = 256
        DENSITY = 0.005
        key = jax.random.key(seed)
        ks = jax.random.split(key, 12)
        x = jax.random.normal(ks[0], (N, D_IN), dtype=jnp.float32)
        adj_a = (jax.random.uniform(ks[1], (N, N)) < DENSITY).astype(jnp.float32)
        adj_b = (jax.random.uniform(ks[2], (N, N)) < DENSITY).astype(jnp.float32)
        W_sa = jax.random.normal(ks[3], (D_IN, D_OUT), dtype=jnp.float32) * (1.414 / np.sqrt(D_IN + D_OUT))
        a_sa = jax.random.normal(ks[4], (1, 2 * D_OUT), dtype=jnp.float32) * (1.414 / np.sqrt(1 + 2 * D_OUT))
        stdv = 1.0 / np.sqrt(D_OUT)
        W_gcnb = jax.random.uniform(ks[5], (D_IN, D_OUT), minval=-stdv, maxval=stdv, dtype=jnp.float32)
        b_gcnb = jax.random.uniform(ks[6], (D_OUT,), minval=-stdv, maxval=stdv, dtype=jnp.float32)
        s = 1.0 / np.sqrt(2 * D_IN)
        Wa = jax.random.uniform(ks[7], (1, 2 * D_IN), minval=-s, maxval=s, dtype=jnp.float32)
        ba = jax.random.uniform(ks[8], (1,), minval=-s, maxval=s, dtype=jnp.float32)
        Wb = jax.random.uniform(ks[9], (1, 2 * D_IN), minval=-s, maxval=s, dtype=jnp.float32)
        bb = jax.random.uniform(ks[10], (1,), minval=-s, maxval=s, dtype=jnp.float32)
        return {'x': x, 'adj_a': adj_a, 'adj_b': adj_b, 'W_sa': W_sa, 'a_sa': a_sa, 'W_gcnb': W_gcnb, 'b_gcnb': b_gcnb, 'Wa': Wa, 'ba': ba, 'Wb': Wb, 'bb': bb}
    _L0_gnn_all = _L0_gnn_setup()
    _L0_gnn_in = {k: v for k, v in _L0_gnn_all.items() if k in ('W_sa', 'a_sa', 'W_gcnb', 'b_gcnb', 'Wa', 'ba', 'Wb', 'bb')}
    del _L0_gnn_all

    def _L1_gnn_setup():
        import jax, jax.numpy as jnp
        import numpy as np
        N = 4096
        DIN = 256
        DOUT = 256
        key = jax.random.key(seed)
        k1, k2, k3 = jax.random.split(key, 3)
        x = jax.random.normal(k1, (N, DIN), dtype=jnp.float32)
        adj = jax.random.uniform(k2, (N, N), dtype=jnp.float32)
        W = jax.random.normal(k3, (DIN, DOUT), dtype=jnp.float32) * (1.0 / np.sqrt(DIN))
        b = jnp.zeros((DOUT,), dtype=jnp.float32)
        return {'x': x, 'adj': adj, 'W': W, 'b': b}
    _L1_gnn_all = _L1_gnn_setup()
    _L1_gnn_in = {k: v for k, v in _L1_gnn_all.items() if k in ('W', 'b')}
    del _L1_gnn_all

    def _L2_gnn_setup():
        import jax, jax.numpy as jnp
        import numpy as np
        N, IN_F, OUT_F = (4096, 256, 256)
        HID = OUT_F // 2
        key = jax.random.key(seed)
        ks = jax.random.split(key, 6)
        x = jax.random.normal(ks[0], (N, IN_F), dtype=jnp.float32)
        adj = jax.random.uniform(ks[1], (N, N), dtype=jnp.float32)
        W1 = jax.random.normal(ks[2], (HID, IN_F), dtype=jnp.float32) * np.sqrt(2.0 / IN_F)
        b1 = jnp.zeros((HID,), dtype=jnp.float32)
        W2 = jax.random.normal(ks[3], (OUT_F, HID), dtype=jnp.float32) * np.sqrt(2.0 / HID)
        b2 = jnp.zeros((OUT_F,), dtype=jnp.float32)
        return {'x': x, 'adj': adj, 'W1': W1, 'b1': b1, 'W2': W2, 'b2': b2}
    _L2_gnn_all = _L2_gnn_setup()
    _L2_gnn_in = {k: v for k, v in _L2_gnn_all.items() if k in ('W1', 'b1', 'W2', 'b2')}
    del _L2_gnn_all

    def _L3_gnn_setup():
        import jax, jax.numpy as jnp
        import numpy as np
        N = 4096
        IN_F = 256
        OUT_F = 256
        key = jax.random.key(seed)
        k1, k2, k3, k4 = jax.random.split(key, 4)
        input = jax.random.normal(k1, (N, IN_F), dtype=jnp.float32)
        adj = jax.random.uniform(k2, (N, N), dtype=jnp.float32)
        W = jax.random.normal(k3, (OUT_F, IN_F), dtype=jnp.float32) / np.sqrt(IN_F)
        b = jax.random.normal(k4, (OUT_F,), dtype=jnp.float32) * 0.01
        return {'input': input, 'adj': adj, 'W': W, 'b': b}
    _L3_gnn_all = _L3_gnn_setup()
    _L3_gnn_in = {k: v for k, v in _L3_gnn_all.items() if k in ('W', 'b')}
    del _L3_gnn_all
    return {'x': x, 'adj': adj, 'L0_gnn_W_sa': _L0_gnn_in['W_sa'], 'L0_gnn_a_sa': _L0_gnn_in['a_sa'], 'L0_gnn_W_gcnb': _L0_gnn_in['W_gcnb'], 'L0_gnn_b_gcnb': _L0_gnn_in['b_gcnb'], 'L0_gnn_Wa': _L0_gnn_in['Wa'], 'L0_gnn_ba': _L0_gnn_in['ba'], 'L0_gnn_Wb': _L0_gnn_in['Wb'], 'L0_gnn_bb': _L0_gnn_in['bb'], 'L1_gnn_W': _L1_gnn_in['W'], 'L1_gnn_b': _L1_gnn_in['b'], 'L2_gnn_W1': _L2_gnn_in['W1'], 'L2_gnn_b1': _L2_gnn_in['b1'], 'L2_gnn_W2': _L2_gnn_in['W2'], 'L2_gnn_b2': _L2_gnn_in['b2'], 'L3_gnn_W': _L3_gnn_in['W'], 'L3_gnn_b': _L3_gnn_in['b']}

def reference(x, adj, L0_gnn_W_sa, L0_gnn_a_sa, L0_gnn_W_gcnb, L0_gnn_b_gcnb, L0_gnn_Wa, L0_gnn_ba, L0_gnn_Wb, L0_gnn_bb, L1_gnn_W, L1_gnn_b, L2_gnn_W1, L2_gnn_b1, L2_gnn_W2, L2_gnn_b2, L3_gnn_W, L3_gnn_b):
    import jax
    import jax.numpy as jnp

    def _L0_gnn_ref(x, adj_a, adj_b, W_sa, a_sa, W_gcnb, b_gcnb, Wa, ba, Wb, bb):
        import jax, jax.numpy as jnp
        import numpy as np
        N = 3072
        D_IN = 256
        D_OUT = 256
        DENSITY = 0.005
        type_sum_a = adj_a @ x
        type_sum_b = adj_b @ x
        attn_a = jax.nn.sigmoid(jnp.concatenate([type_sum_a, x], axis=1) @ Wa.T + ba)
        attn_b = jax.nn.sigmoid(jnp.concatenate([type_sum_b, x], axis=1) @ Wb.T + bb)
        h = x @ W_sa
        Hd = h.shape[1]
        s_left = h @ a_sa[0, :Hd]
        s_right = h @ a_sa[0, Hd:]
        scores = s_left[:, None] + s_right[None, :]
        e = jnp.where(adj_a != 0, jnp.exp(-jax.nn.leaky_relu(scores, 0.01)), 0.0)
        attn = e / (jnp.sum(e, axis=1, keepdims=True) + 1e-05)
        x_a = attn @ h
        x_b = adj_b @ (x @ W_gcnb) + b_gcnb
        return jax.nn.sigmoid(attn_a * x_a + attn_b * x_b)

    def _L1_gnn_ref(x, adj, W, b):
        import jax, jax.numpy as jnp
        import numpy as np
        N = 4096
        DIN = 256
        DOUT = 256
        rowsum = adj.sum(axis=1)
        d_inv_sqrt = jnp.where(rowsum > 0, rowsum ** (-0.5), 0.0)
        normalized_adj = d_inv_sqrt[:, None] * adj * d_inv_sqrt[None, :]
        support = normalized_adj @ x
        out = support @ W + b
        return jax.nn.relu(out)

    def _L2_gnn_ref(x, adj, W1, b1, W2, b2):
        import jax, jax.numpy as jnp
        import numpy as np
        N, IN_F, OUT_F = (4096, 256, 256)
        HID = OUT_F // 2
        h = x @ W1.T + b1
        h = h @ W2.T + b2
        A = adj + jnp.eye(adj.shape[0], dtype=adj.dtype)
        rowsum = A.sum(axis=1)
        r_inv_sqrt = jnp.power(rowsum, -0.5)
        r_inv_sqrt = jnp.where(jnp.isinf(r_inv_sqrt), 0.0, r_inv_sqrt)
        A = r_inv_sqrt[:, None] * A * r_inv_sqrt[None, :]
        return A.astype(jnp.float32) @ h.astype(jnp.float32)

    def _L3_gnn_ref(input, adj, W, b):
        import jax, jax.numpy as jnp
        import numpy as np
        N = 4096
        IN_F = 256
        OUT_F = 256
        h = jnp.einsum('ni,oi->no', input, W) + b
        return adj @ h
    x = _layernorm(x + _L0_gnn_ref(x, adj, adj, L0_gnn_W_sa, L0_gnn_a_sa, L0_gnn_W_gcnb, L0_gnn_b_gcnb, L0_gnn_Wa, L0_gnn_ba, L0_gnn_Wb, L0_gnn_bb), axis=-1)
    x = _layernorm(x + _L1_gnn_ref(x, adj, L1_gnn_W, L1_gnn_b), axis=-1)
    x = _layernorm(x + _L2_gnn_ref(x, adj, L2_gnn_W1, L2_gnn_b1, L2_gnn_W2, L2_gnn_b2), axis=-1)
    x = _layernorm(x + _L3_gnn_ref(x, adj, L3_gnn_W, L3_gnn_b), axis=-1)
    return x

_drawn_inputs = setup_inputs


def setup_inputs(seed=0):
    import zlib

    import numpy as np

    out = dict(_drawn_inputs(seed))
    spreads = {'L1_gnn_b': (0.0, 0.1), 'L2_gnn_b1': (0.0, 0.1), 'L2_gnn_b2': (0.0, 0.1)}
    factors = {'L0_gnn_b_gcnb': 4.568, 'L3_gnn_b': 3.555}
    for name, (base, spread) in spreads.items():
        noise = np.random.default_rng([zlib.crc32(name.encode()), seed]).standard_normal(out[name].shape)
        drawn = base * np.exp(spread * noise) if base else spread * noise
        out[name] = jnp.asarray(drawn.astype(out[name].dtype))
    for name, factor in factors.items():
        out[name] = (out[name] * factor).astype(out[name].dtype)
    return out
```

```python
from contextlib import ExitStack

import concourse.bass as bass
from concourse import mybir

ALU = mybir.AluOpType
ACT = mybir.ActivationFunctionType
F32 = mybir.dt.float32
F16 = mybir.dt.float16
F8 = mybir.dt.float8e4
U8 = mybir.dt.uint8

P = 128
N = 3327
NT = -(-N // P)
PAIRS = NT // 2
D = 256
KC = D // P
HALF = NT // 2
EPS_LN = 1e-5
EPS_ATT = 1e-5
SLOPE = 0.01
SY = 256.0
SAB = 32.0
SM = SAB * SAB
TINY = 1e-30

TRANSPOSE0_AT, PROJECT0_AT = 2, 6
TRANSPOSE_AT, PROJECT_AT = 19, 24

GA = D
ONE = D + 2
WT = D + 3
WTP = D + 4
WM = D + 1
WMP = D + 2
SMALL = 6
WG = D + SMALL


def resnorm_gnn_kernel(nc, adjT, x_rows, x_cols, W_sa, a_sa, W_gcnb, b_gcnb, gate_cols, gate_bias,
                       W1g, b1g, W2a, b2a, W2bT, b2b, W3T, b3, out):
    scratch8 = nc.dram_tensor("adj8", [NT * P * NT * P], U8, kind="Internal").ap()
    a_rows = nc.dram_tensor("a_rows", [NT, P], F32, kind="Internal").ap()

    with ExitStack() as ctx:
        def sb(name, shape, dt):
            return ctx.enter_context(nc.sbuf_tensor(name, shape, dt))

        def ps(name, shape):
            return ctx.enter_context(nc.psum_tensor(name, shape, F32))

        def sem(name):
            return ctx.enter_context(nc.semaphore(name))

        ya = sb("ya", [P, NT, 2, WTP], F16)
        yb = sb("yb", [P, NT, 2, D], F16)
        ym = sb("ym", [P, NT, 2, WMP], F16)
        xres = sb("xres", [P, NT, D], F32)
        cols = sb("cols", [P, NT, 6], F32)
        abcols = sb("abcols", [P, NT, 2], F32)
        adj32 = sb("adj32", [P, 2, NT * P], F32)
        adj8 = sb("adj8_sb", [P, 2, NT * P], F8)
        prod = sb("prod", [P, 2, HALF * P], F32)
        mhi = sb("mhi", [P, 2, NT * P], F16)
        mlo = sb("mlo", [P, 2, NT * P], F16)
        a_bc = sb("a_bc", [P, 2, P], F32)

        wh = sb("wh", [P, KC, D], F32)
        wg = sb("wg", [P, KC, WG], F32)
        w1 = sb("w1", [P, KC, D], F32)
        wc = sb("wc", [P, KC, D], F32)
        w3 = sb("w3", [P, KC, D], F32)
        w2a_sb = sb("w2a_sb", [P, D], F32)
        w2b_sb = sb("w2b_sb", [P, D], F32)
        b1col = sb("b1col", [P, 1], F32)
        b1rep = sb("b1rep", [P, P], F32)
        asa_bc = sb("asa_bc", [P, 2, D], F32)
        bg_bc = sb("bg_bc", [P, D], F32)
        b1_bc = sb("b1_bc", [P, D], F32)
        bc_bc = sb("bc_bc", [P, D], F32)
        b3_bc = sb("b3_bc", [P, D], F32)
        gate_bc = sb("gate_bc", [P, 2], F32)
        ident = sb("ident", [P, P], F32)
        ident16 = sb("ident16", [P, P], F16)
        minus_half = sb("minus_half", [P, 3], F32)

        xT = sb("xT", [P, 2, KC, P], F32)
        xn = sb("xn", [P, 2, D], F32)
        small = sb("small", [P, 2, SMALL], F32)
        ds = sb("ds", [P, 2, 1], F32)
        own = sb("own", [P, 2, 6], F32)
        den = sb("den", [P, 3], F32)
        gates = sb("gates", [P, 2, 2], F32)
        coef = sb("coef", [P, 2, 1], F32)
        escale = sb("escale", [P, 2, 1], F32)
        yscale = sb("yscale", [P, 2, 1], F32)
        t1 = sb("t1", [P, D], F32)
        t3 = sb("t3", [P, D], F32)
        z = sb("z", [P, D], F32)
        sg = sb("sg", [P, D], F32)
        xs = sb("xs", [P, 2, D], F32)
        hb = asa_bc[:, 0, :]
        stats = sb("stats", [P, 7], F32)
        mean_var = sb("mean_var", [P, 2, 2], F32)
        pow_in = sb("pow_in", [P, 2, 3], F32)
        pow_out = sb("pow_out", [P, 2, 3], F32)

        sum_ps = [ps(f"sum_ps{u}", [P, 512]) for u in range(2)]
        att_ps = [ps(f"att_ps{u}", [P, 512]) for u in range(2)]
        tr_ps = ps("tr_ps", [P, KC, P])
        pj_ps = ps("pj_ps", [P, 512])
        idle_ps = ps("idle_ps", [P, 512])

        weights_in = sem("weights_in")
        late_in = sem("late_in")
        x_in = sem("x_in")
        ident_made = sem("ident_made")
        consts_made = sem("consts_made")
        proj_cols_made = sem("proj_cols_made")
        comb_ready = sem("comb_ready")
        comb_done = sem("comb_done")
        comb_saved = sem("comb_saved")
        xT_in = [sem(f"xT_in{u}") for u in range(2)]
        first_proj = sem("first_proj")
        small_ready = sem("small_ready")
        exps_ready = sem("exps_ready")
        ab_ready = sem("ab_ready")
        ds_ready = sem("ds_ready")
        first_hi = sem("first_hi")
        first_lo = sem("first_lo")
        a_out = sem("a_out")
        vec = sem("vec")
        adj32_in = [sem(f"adj32_in{u}") for u in range(2)]
        a_in = [sem(f"a_in{u}") for u in range(2)]
        prod_ready = sem("prod_ready")
        mask_done = sem("mask_done")
        mhi_ready = sem("mhi_ready")
        mlo_ready = sem("mlo_ready")
        cast_done = sem("cast_done")
        adj8_out = [sem(f"adj8_out{u}") for u in range(2)]
        adj8_in = [sem(f"adj8_in{u}") for u in range(2)]
        agg_done = sem("agg_done")
        gate_in = sem("gate_in")
        gate_out = sem("gate_out")
        coef_ready = sem("coef_ready")
        att_scaled = sem("att_scaled")
        z_ready = sem("z_ready")
        sig_ready = sem("sig_ready")
        var_ready = sem("var_ready")
        pow_ready = sem("pow_ready")
        x_ready = sem("x_ready")
        x_saved = sem("x_saved")
        transposed = sem("transposed")
        xT_ready = sem("xT_ready")
        projected = sem("projected")
        hb_ready = sem("hb_ready")
        yscale_ready = sem("yscale_ready")
        sum_read = sem("sum_read")
        hi_ready = sem("hi_ready")
        lo_ready = sem("lo_ready")
        result_out = [sem(f"result_out{u}") for u in range(2)]

        def wait(eng, s, value):
            if not (isinstance(value, int) and value <= 0):
                eng.wait_ge(s, value)

        def count(l, t):
            return l * NT + t + 1

        start_reg = {}

        def tile_of(eng, t):
            start = t * (P * NT * P)
            if not isinstance(t, int):
                if eng not in start_reg:
                    start_reg[eng] = eng.alloc_register("tile_start")
                eng.reg_mov(start_reg[eng], start)
                start = eng.snap(start_reg[eng])
            return scratch8[bass.ds(start, P * NT * P)].rearrange("(p f) -> p f", p=P)

        y_of = [ya, yb, ya, yb]
        w_of = [None, w1, wc, w3]

        block = ctx.enter_context(nc.Block())

        @block.sync
        def _(sp):
            sp.dma_start(wh[:], W_sa).then_inc(weights_in, 16)
            sp.dma_start(wg[:, :, 0:D], W_gcnb).then_inc(weights_in, 16)
            sp.dma_start(wg[:, :, D:D + 4], gate_cols).then_inc(weights_in, 16)
            sp.dma_start(asa_bc[:], a_sa.partition_broadcast(P)).then_inc(weights_in, 16)
            sp.dma_start(gate_bc[:], gate_bias.partition_broadcast(P)).then_inc(weights_in, 16)

            def load_adj32(t, u, p):
                wait(sp, cast_done, t - 1)
                wait(sp, mask_done, 2 * (t - 1))
                sp.dma_start(adj32[:, u, :], adjT[t]).then_inc(adj32_in[u], 16)

            def load_xT(t, u):
                wait(sp, first_proj, t - 1)
                sp.dma_start(xT[:, u], x_cols[t]).then_inc(xT_in[u], 16)

            def store_a(t):
                sp.wait_ge(ab_ready, t + 1)
                sp.dma_start(a_rows[t].rearrange("(p a) -> p a", a=1), abcols[:, t, 0:1]).then_inc(a_out, 16)

            load_xT(0, 0)
            load_xT(1, 1)
            sp.dma_start(w2a_sb[:], W2a).then_inc(late_in, 16)
            sp.dma_start(w2b_sb[:], W2bT).then_inc(late_in, 16)
            sp.dma_start(b1col[:], b2a).then_inc(late_in, 16)
            sp.dma_start(bc_bc[:], b2b.partition_broadcast(P)).then_inc(late_in, 16)
            sp.dma_start(w1[:], W1g).then_inc(late_in, 16)
            sp.dma_start(w3[:], W3T).then_inc(late_in, 16)
            sp.dma_start(bg_bc[:], b_gcnb.partition_broadcast(P)).then_inc(late_in, 16)
            sp.dma_start(b1_bc[:], b1g.partition_broadcast(P)).then_inc(late_in, 16)
            sp.dma_start(b3_bc[:], b3.partition_broadcast(P)).then_inc(late_in, 16)
            load_adj32(0, 0, 0)
            load_adj32(1, 1, 0)
            sp.dma_start(xres[:], x_rows).then_inc(x_in, 16)
            with sp.Fori(1, PAIRS) as p:
                for u in range(2):
                    store_a(2 * p + u - 2)
                    load_xT(2 * p + u, u)
            for t in range(NT - 2, NT):
                store_a(t)

            def load_a(t, u):
                wait(sp, prod_ready, 2 * (t - 1))
                sp.dma_start(a_bc[:, u, :], a_rows[t].partition_broadcast(P)).then_inc(a_in[u], 16)

            sp.wait_ge(a_out, 16 * NT)
            load_a(0, 0)
            load_a(1, 1)

            def layer0(t, u, p, ahead=True):
                dst = tile_of(sp, t)
                sp.wait_ge(cast_done, t + 1)
                sp.dma_start(dst, adj8[:, u, :].bitcast(U8)).then_inc(adj8_out[u], 16)
                if ahead:
                    load_a(t + 2, u)
                    load_adj32(t + 2, u, p + 1)

            with sp.Fori(0, PAIRS - 1) as p:
                for u in range(2):
                    layer0(2 * p + u, u, p)
            for u in range(2):
                layer0(NT - 2 + u, u, PAIRS - 1, False)

            for u in range(2):
                sp.wait_ge(adj8_out[u], 16 * PAIRS)
            for l in range(1, 4):
                with sp.Fori(0, PAIRS) as p:
                    for u in range(2):
                        t = 2 * p + u
                        src = tile_of(sp, t)
                        sp.wait_ge(agg_done, count(l, t - 2))
                        sp.dma_start(adj8[:, u, :].bitcast(U8), src).then_inc(adj8_in[u], 16)

        @block.scalar
        def _(act):
            def first(t, u):
                act.wait_ge(small_ready, t + 1)
                nc.scalar.activation(abcols[:, t, :], small[:, u, 4:6], ACT.Exp,
                                     scale=-(1.0 - SLOPE))
                nc.scalar.activation(cols[:, t, 0:2], small[:, u, 4:6], ACT.Exp,
                                     scale=-SLOPE).then_inc(exps_ready, 1)
                nc.scalar.activation(ya[:, t, 0, 0:ONE], sum_ps[u][:, 0:ONE], ACT.Copy,
                                     scale=SY)
                act.wait_ge(ds_ready, t + 1)
                nc.scalar.activation(ym[:, t, 0, 0:D], att_ps[u][:, 0:D], ACT.Copy,
                                     scale=ds[:, u, :]).then_inc(first_hi, 1)

            with act.Fori(0, PAIRS) as p:
                for u in range(2):
                    first(2 * p + u, u)

            def wait_for_cast(t, u, p):
                act.wait_ge(adj32_in[u], 16 * (p + 1))
                wait(act, agg_done, t - 1)
                wait(act, adj8_out[u], 16 * p)

            def cast(t, u):
                nc.scalar.copy(adj8[:, u, :], adj32[:, u, :], saturate=False).then_inc(cast_done, 1)

            def high_part(t, u, h):
                act.wait_ge(mask_done, 2 * t + h + 1)
                if h == 0:
                    wait(act, agg_done, t - 1)
                nc.scalar.copy(mhi[:, u, h * HALF * P:(h + 1) * HALF * P],
                               prod[:, h, :]).then_inc(mhi_ready, 1)

            def epilogue0(t, v):
                act.wait_ge(gate_in, t + 1)
                nc.scalar.activation(gates[:, v, :], gates[:, v, :], ACT.Sigmoid).then_inc(gate_out, 1)
                act.wait_ge(coef_ready, t + 1)
                nc.scalar.activation(t3[:], att_ps[v][:, 0:D], ACT.Copy,
                                     scale=coef[:, v, :]).then_inc(att_scaled, 1)
                act.wait_ge(z_ready, t + 1)
                nc.scalar.activation(sg[:], z[:], ACT.Sigmoid).then_inc(sig_ready, 1)

            def next_rows(l, t, v):
                act.wait_ge(transposed, count(l, t))
                nc.scalar.copy(xT[:, v], tr_ps[:]).then_inc(xT_ready, 1)
                act.wait_ge(projected, count(l, t))
                dst = y_of[l + 1][:, t, 0, 0:D]
                if l < 2:
                    act.wait_ge(yscale_ready, count(l, t))
                if l == 0:
                    nc.scalar.activation(dst, pj_ps[:, 0:D], ACT.Copy,
                                         scale=yscale[:, v, :]).then_inc(hi_ready, 1)
                elif l == 1:
                    act.wait_ge(hb_ready, t + 1)
                    nc.scalar.activation(dst, hb, ACT.Copy, scale=yscale[:, v, :]).then_inc(hi_ready, 1)
                else:
                    act.wait_ge(hb_ready, NT + t + 1)
                    nc.scalar.activation(dst, hb, ACT.Copy, scale=SY).then_inc(hi_ready, 1)

            def window0(t, u, p, ahead=True):
                v = 1 - u
                has_prev = not (isinstance(t, int) and t == 0)
                if ahead:
                    wait_for_cast(t + 1, v, p + u)
                if has_prev:
                    epilogue0(t - 1, v)
                if ahead:
                    cast(t + 1, v)
                    high_part(t + 1, v, 0)
                if has_prev:
                    next_rows(0, t - 1, v)
                if ahead:
                    high_part(t + 1, v, 1)

            wait_for_cast(0, 0, 0)
            cast(0, 0)
            high_part(0, 0, 0)
            high_part(0, 0, 1)
            for u in range(2):
                window0(u, u, 0)
            with act.Fori(1, PAIRS - 1) as p:
                for u in range(2):
                    window0(2 * p + u, u, p)
            for u in range(2):
                window0(NT - 2 + u, u, PAIRS - 1, ahead=(u == 0))

            epilogue0(NT - 1, 1)
            next_rows(0, NT - 1, 1)
            for l in range(1, 3):
                with act.Fori(0, PAIRS) as p:
                    for v in range(2):
                        next_rows(l, 2 * p + v, v)

        @block.gpsimd
        def _(pool):
            nc.gpsimd.memset(minus_half[:], -0.5).then_inc(consts_made, 1)
            nc.gpsimd.memset(ident[:], 0.0).then_inc(ident_made, 1)
            pool.wait_ge(ident_made, 1)
            nc.gpsimd.affine_select(out=ident[:], in_=ident[:], compare_op=ALU.not_equal, fill=1.0, base=0,
                                    pattern=[[-1, P]], channel_multiplier=1).then_inc(ident_made, 1)
            pool.wait_ge(ident_made, 2)
            nc.gpsimd.tensor_copy(ident16[:], ident[:]).then_inc(ident_made, 1)
            nc.gpsimd.memset(ya[:, :, 0, ONE:ONE + 1], 1.0).then_inc(ident_made, 1)
            pool.wait_ge(consts_made, 1)

            def product(t, u, h, p):
                if h == 0:
                    pool.wait_ge(a_in[u], 16 * (p + 1))
                wait(pool, mlo_ready, 2 * (t - 1) + h + 1)
                wait(pool, mhi_ready, 2 * (t - 1) + h + 1)
                b = abcols[:, h * HALF:(h + 1) * HALF, 1:2].broadcast_to([P, HALF, P])
                a = a_bc[:, u:u + 1, :].broadcast_to([P, HALF, P])
                nc.gpsimd.tensor_tensor(prod[:, h, :].rearrange("p (j i) -> p j i", i=P), a, b,
                                        ALU.mult).then_inc(prod_ready, 1)

            def power(l, t, v):
                n = 3 if l == 0 else 1
                pool.wait_ge(var_ready, count(l, t))
                nc.gpsimd.tensor_tensor(pow_out[:, v, 0:n], pow_in[:, v, 0:n], minus_half[:, 0:n],
                                        ALU.pow).then_inc(pow_ready, 1)

            def save_x(l, t, v):
                pool.wait_ge(x_ready, count(l, t))
                nc.gpsimd.tensor_copy(xres[:, t, :], xn[:, v, :]).then_inc(x_saved, 1)

            def window0(t, u, p, ahead=2):
                v = 1 - u
                if not (isinstance(t, int) and t == 0):
                    power(0, t - 1, v)
                if ahead >= 1:
                    product(t + 1, v, 1, p + u)
                if not (isinstance(t, int) and t == 0):
                    save_x(0, t - 1, v)
                if ahead >= 2:
                    product(t + 2, u, 0, p + 1)

            pool.wait_ge(ab_ready, NT)
            product(0, 0, 0, 0)
            product(0, 0, 1, 0)
            product(1, 1, 0, 0)
            for u in range(2):
                window0(u, u, 0)
            with pool.Fori(1, PAIRS - 1) as p:
                for u in range(2):
                    window0(2 * p + u, u, p)
            window0(NT - 2, 0, PAIRS - 1, 1)
            window0(NT - 1, 1, PAIRS - 1, 0)
            power(0, NT - 1, 1)
            save_x(0, NT - 1, 1)
            for l in range(1, 4):
                with pool.Fori(0, PAIRS) as p:
                    for v in range(2):
                        t = 2 * p + v
                        power(l, t, v)
                        if l < 3:
                            save_x(l, t, v)
                        else:
                            pool.wait_ge(x_ready, count(l, t))
                            pool.dma_start(out[t], xn[:, v, :]).then_inc(result_out[v], 16)
            for v in range(2):
                pool.wait_ge(result_out[v], 16 * PAIRS)

        @block.vector
        def _(dve):
            done = [0]

            def link(ins):
                done[0] = done[0] + 1
                ins.then_inc(vec, 1)

            def linked():
                dve.wait_ge(vec, done[0])

            dve.wait_ge(weights_in, 16 * 5)
            for c in range(KC):
                for side in range(2):
                    nc.vector.tensor_tensor_reduce(
                        out=(t1, t3, z, sg)[2 * c + side][:], in0=wh[:, c, :], in1=asa_bc[:, side, :], scale=1.0, scalar=0.0,
                        op0=ALU.mult, op1=ALU.add,
                        accum_out=wg[:, c, D + 4 + side:D + 5 + side]).then_inc(proj_cols_made, 1)

            def first(t, u):
                dve.wait_ge(first_proj, t + 1)
                nc.vector.tensor_copy(small[:, u, :], sum_ps[u][:, D:WG]).then_inc(small_ready, 1)
                dve.wait_ge(exps_ready, t + 1)
                nc.vector.tensor_scalar(ds[:, u, :], cols[:, t, 1:2], SY, None, ALU.mult).then_inc(ds_ready, 1)
                nc.vector.tensor_scalar(abcols[:, t, :], abcols[:, t, :], SAB, None, ALU.mult).then_inc(ab_ready, 1)
                nc.vector.tensor_tensor(cols[:, t, 2:4], small[:, u, 2:4], gate_bc[:], ALU.add)
                dve.wait_ge(ds_ready, t + 1)
                link(nc.vector.tensor_copy(ym[:, t, 0, D:WM], ds[:, u, :]))
                dve.wait_ge(first_hi, t + 1)
                nc.vector.scalar_tensor_tensor(ya[:, t, 1, 0:ONE], sum_ps[u][:, 0:ONE], SY, ya[:, t, 0, 0:ONE],
                                               ALU.mult, ALU.subtract)
                linked()
                nc.vector.tensor_tensor(ym[:, t, 1, D:WM], ds[:, u, :], ym[:, t, 0, D:WM], ALU.subtract)
                nc.vector.scalar_tensor_tensor(ym[:, t, 1, 0:D], att_ps[u][:, 0:D], ds[:, u, :], ym[:, t, 0, 0:D],
                                               ALU.mult, ALU.subtract).then_inc(first_lo, 1)

            with dve.Fori(0, PAIRS) as p:
                for u in range(2):
                    done[0] = 2 * p + u
                    first(2 * p + u, u)
            done[0] = NT

            dve.wait_ge(late_in, 16 * 9)
            link(nc.vector.memset(b1rep[:], 1.0))
            linked()
            nc.vector.tensor_scalar(b1rep[:], b1rep[:], b1col[:], None, ALU.mult).then_inc(comb_ready, 1)
            dve.wait_ge(comb_done, 1)
            nc.vector.tensor_copy(wc[:, 0, :], sum_ps[0][:, 0:D]).then_inc(comb_saved, 1)
            nc.vector.tensor_copy(wc[:, 1, :], sum_ps[1][:, 0:D]).then_inc(comb_saved, 1)
            nc.vector.tensor_tensor(bc_bc[:], att_ps[0][:, 0:D], bc_bc[:], ALU.add).then_inc(comb_saved, 1)
            base0 = NT + 1

            def attention(t, u, h, p):
                dve.wait_ge(prod_ready, 2 * t + h + 1)
                if h == 0:
                    dve.wait_ge(adj32_in[u], 16 * (p + 1))
                part = slice(h * HALF * P, (h + 1) * HALF * P)
                nc.vector.scalar_tensor_tensor(prod[:, h, :], prod[:, h, :], SM, adj32[:, u, part],
                                               ALU.min, ALU.mult).then_inc(mask_done, 1)
                dve.wait_ge(mhi_ready, 2 * t + h + 1)
                nc.vector.tensor_tensor(mlo[:, u, part], prod[:, h, :], mhi[:, u, part],
                                        ALU.subtract).then_inc(mlo_ready, 1)

            def layernorm(l, t, v):
                link(nc.vector.bn_stats(stats[:, 0:6], xs[:, v, :]))
                linked()
                nc.vector.tensor_copy(stats[:, 6:7], stats[:, 0:1])
                link(nc.vector.bn_aggr(mean_var[:, v, :], stats[:, 0:6]))
                linked()
                nc.vector.tensor_scalar(pow_in[:, v, 0:1], mean_var[:, v, 1:2], EPS_LN, None,
                                        ALU.add).then_inc(var_ready, 1)
                dve.wait_ge(pow_ready, count(l, t))
                if l in (1, 2):
                    wait(dve, transposed, count(l, t - 2))
                    wait(dve, x_saved, count(l, t - 2))
                nc.vector.tensor_scalar(xn[:, v, :], xs[:, v, :], mean_var[:, v, 0:1], pow_out[:, v, 0:1],
                                        ALU.subtract, ALU.mult).then_inc(x_ready, 1)

            LINKS0 = 8

            def epilogue0(t, v):
                done[0] = base0 + LINKS0 * t
                T, M = sum_ps[v], att_ps[v]
                link(nc.vector.tensor_copy(own[:, v, 0:4], cols[:, t, 0:4]))
                dve.wait_ge(agg_done, t + 1)
                linked()
                nc.vector.scalar_tensor_tensor(gates[:, v, :], T[:, GA:GA + 2], 1.0 / SY, own[:, v, 2:4],
                                               ALU.mult, ALU.add).then_inc(gate_in, 1)
                link(nc.vector.tensor_scalar(den[:, 0:1], M[:, D:WM], own[:, v, 0:1], EPS_ATT * SM * SY,
                                             ALU.mult, ALU.add))
                linked()
                link(nc.vector.reciprocal(den[:, 1:2], den[:, 0:1]))
                link(nc.vector.scalar_tensor_tensor(t1[:], T[:, 0:D], 1.0 / SY, bg_bc[:], ALU.mult, ALU.add))
                dve.wait_ge(gate_out, t + 1)
                linked()
                nc.vector.scalar_tensor_tensor(coef[:, v, :], den[:, 1:2], own[:, v, 0:1], gates[:, v, 0:1],
                                               ALU.mult, ALU.mult).then_inc(coef_ready, 1)
                nc.vector.tensor_scalar(pow_in[:, v, 1:2], T[:, ONE:WT], TINY, None, ALU.max)
                nc.vector.tensor_scalar(pow_in[:, v, 2:3], T[:, ONE:WT], 1.0, TINY, ALU.add, ALU.max)
                link(nc.vector.tensor_scalar(den[:, 2:3], T[:, ONE:WT], 0.0, None, ALU.is_gt))
                dve.wait_ge(att_scaled, t + 1)
                nc.vector.scalar_tensor_tensor(z[:], t1[:], gates[:, v, 1:2], t3[:],
                                               ALU.mult, ALU.add).then_inc(z_ready, 1)
                dve.wait_ge(sig_ready, t + 1)
                if isinstance(t, int) and t == 0:
                    dve.wait_ge(x_in, 16)
                link(nc.vector.tensor_tensor(xs[:, v, :], sg[:], xres[:, t, :], ALU.add))
                linked()
                layernorm(0, t, v)
                nc.vector.tensor_tensor(cols[:, t, 4:5], pow_out[:, v, 1:2], den[:, 2:3], ALU.mult)
                nc.vector.tensor_copy(cols[:, t, 5:6], pow_out[:, v, 2:3])
                nc.vector.scalar_tensor_tensor(yscale[:, v, :], pow_out[:, v, 1:2], SY, den[:, 2:3],
                                               ALU.mult, ALU.mult).then_inc(yscale_ready, 1)

            def rows(l, t, v):
                y = y_of[l + 1]
                dve.wait_ge(projected, count(l, t))
                if l < 2:
                    dve.wait_ge(yscale_ready, count(l, t))
                if l == 0:
                    dve.wait_ge(hi_ready, count(l, t))
                    nc.vector.scalar_tensor_tensor(y[:, t, 1, 0:D], pj_ps[:, 0:D], yscale[:, v, :],
                                                   y[:, t, 0, 0:D], ALU.mult, ALU.subtract).then_inc(lo_ready, 1)
                else:
                    nc.vector.tensor_tensor(hb, pj_ps[:, 0:D], (bc_bc if l == 1 else b3_bc)[:],
                                            ALU.add).then_inc(hb_ready, 1)
                    dve.wait_ge(hi_ready, count(l, t))
                    nc.vector.scalar_tensor_tensor(y[:, t, 1, 0:D], hb, yscale[:, v, :] if l == 1 else SY,
                                                   y[:, t, 0, 0:D], ALU.mult, ALU.subtract).then_inc(lo_ready, 1)

            LINKS, LINKS3 = 5, 3

            def epilogue(l, t, v):
                done[0] = base0 + LINKS0 * NT + LINKS * (NT * (l - 1) + t)
                A = sum_ps[v]
                link(nc.vector.tensor_copy(own[:, v, 4:6], cols[:, t, 4:6]))
                linked()
                if l == 1:
                    link(nc.vector.tensor_scalar(escale[:, v, :], own[:, v, 4:5], 1.0 / SY, None, ALU.mult))
                    nc.vector.tensor_scalar(yscale[:, v, :], own[:, v, 5:6], SY, None,
                                            ALU.mult).then_inc(yscale_ready, 1)
                else:
                    link(nc.vector.tensor_scalar(escale[:, v, :], own[:, v, 5:6], 1.0 / SY, None, ALU.mult))
                linked()
                dve.wait_ge(agg_done, count(l, t))
                wait(dve, x_saved, count(l - 1, t))
                if l == 1:
                    nc.vector.scalar_tensor_tensor(t1[:], A[:, 0:D], escale[:, v, :], b1_bc[:],
                                                   ALU.mult, ALU.add).then_inc(sum_read, 1)
                    dve.wait_ge(sum_read, t + 1)
                    link(nc.vector.scalar_tensor_tensor(xs[:, v, :], t1[:], 0.0, xres[:, t, :], ALU.max, ALU.add))
                else:
                    link(nc.vector.scalar_tensor_tensor(xs[:, v, :], A[:, 0:D], escale[:, v, :],
                                                        xres[:, t, :], ALU.mult, ALU.add))
                linked()
                layernorm(l, t, v)

            def epilogue3(t, v, p):
                done[0] = base0 + LINKS0 * NT + LINKS * NT * 2 + LINKS3 * t
                dve.wait_ge(agg_done, count(3, t))
                dve.wait_ge(x_ready, count(3, t - 2))
                dve.wait_ge(x_saved, count(2, t))
                link(nc.vector.scalar_tensor_tensor(xs[:, v, :], sum_ps[v][:, 0:D], 1.0 / SY, xres[:, t, :],
                                                    ALU.mult, ALU.add))
                linked()
                wait(dve, result_out[v], 16 * p)
                if isinstance(t, int):
                    dve.wait_ge(transposed, count(2, NT - 1))
                    dve.wait_ge(x_saved, count(2, NT - 1))
                layernorm(3, t, v)

            def window0(t, u, p, ahead=True):
                v = 1 - u
                has_prev = not (isinstance(t, int) and t == 0)
                if has_prev:
                    epilogue0(t - 1, v)
                if ahead:
                    attention(t + 1, v, 0, p + u)
                if has_prev:
                    rows(0, t - 1, v)
                if ahead:
                    attention(t + 1, v, 1, p + u)

            attention(0, 0, 0, 0)
            attention(0, 0, 1, 0)
            for u in range(2):
                window0(u, u, 0)
            with dve.Fori(1, PAIRS - 1) as p:
                for u in range(2):
                    window0(2 * p + u, u, p)
            for u in range(2):
                window0(NT - 2 + u, u, PAIRS - 1, ahead=(u == 0))
            epilogue0(NT - 1, 1)
            rows(0, NT - 1, 1)

            def turn(l, p, first=False):
                for v in range(2):
                    t = 2 * p + v
                    if l < 3:
                        epilogue(l, t, v)
                    else:
                        epilogue3(t, v, p)
                    if l < 3 and not (first and v == 0):
                        rows(l, t - 1, 1 - v)

            for l in range(1, 4):
                turn(l, 0, True)
                with dve.Fori(1, PAIRS) as p:
                    turn(l, p)
                if l < 3:
                    rows(l, NT - 1, 1)

        @block.tensor
        def _(pe):
            pe.wait_ge(weights_in, 16 * 5)
            pe.wait_ge(proj_cols_made, 2 * KC)

            def first(t, u, p):
                pe.wait_ge(xT_in[u], 16 * (p + 1))
                wait(pe, first_lo, t - 1)
                for c in range(KC):
                    nc.tensor.matmul(sum_ps[u][:, 0:WG], xT[:, u, c, :], wg[:, c, :],
                                     start=(c == 0), stop=(c == KC - 1))
                for c in range(KC):
                    last = nc.tensor.matmul(att_ps[u][:, 0:D], xT[:, u, c, :], wh[:, c, :],
                                            start=(c == 0), stop=(c == KC - 1))
                last.then_inc(first_proj, 1)

            for u in range(2):
                first(u, u, 0)
            with pe.Fori(1, PAIRS) as p:
                for u in range(2):
                    first(2 * p + u, u, p)

            pe.wait_ge(comb_ready, 1)
            pe.wait_ge(late_in, 16 * 9)
            pe.wait_ge(first_lo, NT)
            for c in range(KC):
                nc.tensor.matmul(sum_ps[c][:, 0:D], w2a_sb[:, c * P:(c + 1) * P], w2b_sb[:], start=True, stop=True)
            nc.tensor.matmul(att_ps[0][:, 0:D], b1rep[:], w2b_sb[:], start=True, stop=True).then_inc(comb_done, 1)
            pe.wait_ge(comb_saved, 3)
            pe.wait_ge(ident_made, 4)

            def transpose(l, t, v):
                pe.wait_ge(x_ready, count(l, t))
                wait(pe, xT_ready, count(l, t) - 1)
                for c in range(KC):
                    last = nc.tensor.transpose(tr_ps[:, c, :], xn[:, v, c * P:(c + 1) * P], ident[:])
                last.then_inc(transposed, 1)

            def project(l, t, v):
                pe.wait_ge(xT_ready, count(l, t))
                wait(pe, lo_ready, count(l, t) - 1)
                for c in range(KC):
                    last = nc.tensor.matmul(pj_ps[:, 0:D], xT[:, v, c, :], w_of[l + 1][:, c, :],
                                            start=(c == 0), stop=(c == KC - 1))
                last.then_inc(projected, 1)

            def window0(t, u):
                v = 1 - u
                has_prev = not (isinstance(t, int) and t == 0)
                wait(pe, x_ready, t - 1)
                pe.wait_ge(cast_done, t + 1)
                for j in range(NT):
                    if j % HALF == 0:
                        pe.wait_ge(mlo_ready, 2 * t + j // HALF + 1)
                    hi, lo = mhi[:, u, j * P:(j + 1) * P], mlo[:, u, j * P:(j + 1) * P]
                    nc.tensor.matmul(att_ps[u][:, 0:WM], hi, ym[:, j, 0, 0:WM], start=(j == 0), stop=False)
                    nc.tensor.matmul(att_ps[u][:, 0:WM], hi, ym[:, j, 1, 0:WM], start=False, stop=False)
                    nc.tensor.matmul(att_ps[u][:, 0:WM], lo, ym[:, j, 0, 0:WM], start=False, stop=(j == NT - 1))
                for j in range(NT):
                    if has_prev and j == TRANSPOSE0_AT:
                        transpose(0, t - 1, v)
                    if has_prev and j == PROJECT0_AT:
                        project(0, t - 1, v)
                    w = adj8[:, u, j * P:(j + 1) * P]
                    nc.tensor.matmul(sum_ps[u][:, 0:WT], w, ya[:, j, 0, 0:WT], start=(j == 0), stop=False)
                    last = nc.tensor.matmul(sum_ps[u][:, 0:ONE], w, ya[:, j, 1, 0:ONE], start=False,
                                            stop=(j == NT - 1))
                last.then_inc(agg_done, 1)

            for u in range(2):
                window0(u, u)
            with pe.Fori(1, PAIRS) as p:
                for u in range(2):
                    window0(2 * p + u, u)

            def window(l, t, u, p):
                v = 1 - u
                y = y_of[l]
                starts = isinstance(t, int) and t == 0
                pe.wait_ge(x_ready, count(l, t - 2))
                pe.wait_ge(adj8_in[u], 16 * (PAIRS * (l - 1) + p + 1))
                if l == 2:
                    if starts:
                        pe.wait_ge(lo_ready, count(1, 0))
                    nc.tensor.matmul(sum_ps[u][:, 0:D], ident16[:], y[:, t, 0, 0:D], start=True, stop=False)
                    nc.tensor.matmul(sum_ps[u][:, 0:D], ident16[:], y[:, t, 1, 0:D], start=False, stop=False)
                else:
                    nc.tensor.matmul(idle_ps[:, 0:1], ident16[:], ident16[:, 0:1], start=True, stop=True)
                for j in range(NT):
                    if j == TRANSPOSE_AT:
                        if starts:
                            transpose(l - 1, NT - 1, v)
                        elif l < 3:
                            transpose(l, t - 1, v)
                    if j == PROJECT_AT:
                        if starts:
                            project(l - 1, NT - 1, v)
                        elif l < 3:
                            project(l, t - 1, v)
                    if starts:
                        pe.wait_ge(lo_ready, count(l - 1, j))
                    w = adj8[:, u, j * P:(j + 1) * P]
                    nc.tensor.matmul(sum_ps[u][:, 0:D], w, y[:, j, 0, 0:D], start=(l != 2 and j == 0), stop=False)
                    last = nc.tensor.matmul(sum_ps[u][:, 0:D], w, y[:, j, 1, 0:D], start=False, stop=(j == NT - 1))
                last.then_inc(agg_done, 1)

            for l in range(1, 4):
                for u in range(2):
                    window(l, u, u, 0)
                with pe.Fori(1, PAIRS) as p:
                    for u in range(2):
                        window(l, 2 * p + u, u, p)




def kernel(**inputs):
    import numpy as np
    import concourse.bacc as bacc
    from concourse.bass_utils import run_bass_kernel_spmd as run

    v = {k: np.ascontiguousarray(a) for k, a in inputs.items()}
    pad = NT * P - N

    adjT = np.pad(v["adj"], ((0, pad), (0, pad))).reshape(NT, P, NT, P)
    xp = np.pad(v["x"], ((0, pad), (0, 0))).reshape(NT, P, D)
    chunks = lambda w: w.reshape(KC, P, -1).transpose(1, 0, 2)
    wa, wb = v["L0_gnn_Wa"].reshape(2, D), v["L0_gnn_Wb"].reshape(2, D)
    arrays = {
        "adjT": adjT.transpose(0, 3, 2, 1).reshape(NT, P, NT * P),
        "x_rows": xp.transpose(1, 0, 2),
        "x_cols": xp.reshape(NT, P, KC, P).transpose(0, 3, 2, 1),
        "W_sa": chunks(v["L0_gnn_W_sa"]),
        "a_sa": v["L0_gnn_a_sa"].reshape(2, D),
        "W_gcnb": chunks(v["L0_gnn_W_gcnb"]),
        "b_gcnb": v["L0_gnn_b_gcnb"],
        "gate_cols": chunks(np.stack([wa[0], wb[0], wa[1], wb[1]], axis=1)),
        "gate_bias": np.concatenate([v["L0_gnn_ba"], v["L0_gnn_bb"]]),
        "W1g": chunks(v["L1_gnn_W"]),
        "b1g": v["L1_gnn_b"],
        "W2a": v["L2_gnn_W1"],
        "b2a": v["L2_gnn_b1"].reshape(P, 1),
        "W2bT": v["L2_gnn_W2"].T,
        "b2b": v["L2_gnn_b2"],
        "W3T": chunks(v["L3_gnn_W"].T),
        "b3": v["L3_gnn_b"],
    }
    nc = bacc.Bacc("TRN2", target_bir_lowering=False, num_devices=1)
    arrays = {k: np.ascontiguousarray(a) for k, a in arrays.items()}
    aps = [nc.dram_tensor(k, a.shape, mybir.dt.from_np(a.dtype), kind="ExternalInput").ap()
           for k, a in arrays.items()]
    out = nc.dram_tensor("out", (NT, P, D), F32, kind="ExternalOutput").ap()
    resnorm_gnn_kernel(nc, *aps, out)
    r = run(nc, [arrays], core_ids=[0])
    return r.results[0]["out"].reshape(NT * P, D)[:N]
```

```python
from contextlib import ExitStack

import concourse.bass as bass
from concourse import mybir

ALU = mybir.AluOpType
ACT = mybir.ActivationFunctionType
F32 = mybir.dt.float32
F16 = mybir.dt.float16
F8 = mybir.dt.float8e4
U8 = mybir.dt.uint8

P = 128
N = 3327
NT = -(-N // P)
PAIRS = NT // 2
D = 256
KC = D // P
HALF = NT // 2
MIDDLE = 3
EPS_LN = 1e-5
EPS_ATT = 1e-5
SLOPE = 0.01
SY = 256.0
SX = 256.0
SW = 256.0
SAB = 32.0
SM = SAB * SAB
TINY = 1e-30

TRANSPOSE0_AT, PROJECT0_AT = 3, 14
TRANSPOSE_AT, PROJECT_AT = 18, 24

GA = D
ONE = D + 2
WT = D + 3
WTP = D + 4
WM = D + 1
WMP = D + 2
SMALL = 6
WG = D + SMALL


def resnorm_gnn_kernel(nc, adjT, x_rows, x_cols, W_sa, a_sa, W_gcnb, b_gcnb, gate_cols, gate_bias,
                       W1g, b1g, W2a, b2a, W2bT, b2b, W3T, b3, out):
    scratch8 = nc.dram_tensor("adj8", [NT * P * NT * P], U8, kind="Internal").ap()
    a_rows = nc.dram_tensor("a_rows", [NT, P], F32, kind="Internal").ap()

    with ExitStack() as ctx:
        def sb(name, shape, dt):
            return ctx.enter_context(nc.sbuf_tensor(name, shape, dt))

        def ps(name, shape):
            return ctx.enter_context(nc.psum_tensor(name, shape, F32))

        def sem(name):
            return ctx.enter_context(nc.semaphore(name))

        ya = sb("ya", [P, NT, 2, WTP], F16)
        yb = sb("yb", [P, NT, 2, D], F16)
        ym = sb("ym", [P, NT, 2, WMP], F16)
        xres = sb("xres", [P, NT, D], F32)
        cols = sb("cols", [P, NT, 6], F32)
        abcols = sb("abcols", [P, NT, 2], F32)
        adj32 = sb("adj32", [P, 2, NT * P], F32)
        adj8 = sb("adj8_sb", [P, 2, NT * P], F8)
        prod = sb("prod", [P, 2, HALF * P], F32)
        mhi = sb("mhi", [P, 2, NT * P], F16)
        mlo = sb("mlo", [P, 2, NT * P], F16)
        a_bc = sb("a_bc", [P, 2, P], F32)

        wh = sb("wh", [P, KC, D], F32)
        wg = sb("wg", [P, KC, WG], F32)
        w16 = sb("w16", [P, 3, KC, 2, D], F16)
        staged = mlo[:, 1, :].bitcast(F32)
        w1 = staged[:, 0:KC * D].rearrange("p (c n) -> p c n", c=KC)
        w3 = staged[:, KC * D:2 * KC * D].rearrange("p (c n) -> p c n", c=KC)
        w2a_sb = staged[:, 2 * KC * D:2 * KC * D + D]
        w2b_sb = staged[:, 2 * KC * D + D:2 * KC * D + 2 * D]
        b1col = sb("b1col", [P, 1], F32)
        b1rep = sb("b1rep", [P, P], F32)
        asa_bc = sb("asa_bc", [P, 2, D], F32)
        bg_bc = sb("bg_bc", [P, D], F32)
        b1_bc = sb("b1_bc", [P, D], F32)
        bc_bc = sb("bc_bc", [P, D], F32)
        b3_bc = sb("b3_bc", [P, D], F32)
        gate_bc = sb("gate_bc", [P, 2], F32)
        ident = sb("ident", [P, P], F32)
        ident16 = sb("ident16", [P, P], F16)
        minus_half = sb("minus_half", [P, 3], F32)

        xT = mhi[:, 0, 0:4 * KC * P * 2].bitcast(F32).rearrange("p (b c i) -> p b c i", b=4, c=KC)
        xTh = sb("xTh", [P, 2, KC, P], F16)
        xTl = sb("xTl", [P, 2, KC, P], F16)
        xn = sb("xn", [P, 2, D], F32)
        small = sb("small", [P, 2, SMALL], F32)
        ds = sb("ds", [P, 2, 1], F32)
        own = sb("own", [P, 2, 6], F32)
        den = sb("den", [P, 3], F32)
        gates = sb("gates", [P, 2, 2], F32)
        coef = sb("coef", [P, 2, 1], F32)
        escale = sb("escale", [P, 2, 1], F32)
        yscale = sb("yscale", [P, 2, 1], F32)
        t1 = sb("t1", [P, D], F32)
        t3 = sb("t3", [P, D], F32)
        z = sb("z", [P, D], F32)
        sg = sb("sg", [P, D], F32)
        xs = sb("xs", [P, 2, D], F32)
        hb = asa_bc[:, 0, :]
        stats = sb("stats", [P, 7], F32)
        mean_var = sb("mean_var", [P, 2, 2], F32)
        pow_in = sb("pow_in", [P, 2, 3], F32)
        pow_out = sb("pow_out", [P, 2, 3], F32)

        sum_ps = [ps(f"sum_ps{u}", [P, 512]) for u in range(2)]
        att_ps = [ps(f"att_ps{u}", [P, 512]) for u in range(2)]
        tr_ps = ps("tr_ps", [P, KC, P])
        pj_ps = ps("pj_ps", [P, 512])
        idle_ps = ps("idle_ps", [P, 512])

        weights_in = sem("weights_in")
        late_in = sem("late_in")
        x_in = sem("x_in")
        ident_made = sem("ident_made")
        consts_made = sem("consts_made")
        proj_cols_made = sem("proj_cols_made")
        comb_ready = sem("comb_ready")
        comb_done = sem("comb_done")
        comb_saved = sem("comb_saved")
        xT_in = [sem(f"xT_in{b}") for b in range(4)]
        sums_projected = sem("sums_projected")
        h_projected = sem("h_projected")
        small_ready = sem("small_ready")
        exps_ready = sem("exps_ready")
        ab_ready = sem("ab_ready")
        ds_ready = sem("ds_ready")
        sums_hi = sem("sums_hi")
        sums_lo = sem("sums_lo")
        h_hi = sem("h_hi")
        h_lo = sem("h_lo")
        w16_hi = sem("w16_hi")
        w16_ready = sem("w16_ready")
        xT_hi = sem("xT_hi")
        a_out = sem("a_out")
        a_out_first = sem("a_out_first")
        vec = sem("vec")
        adj32_in = [sem(f"adj32_in{u}") for u in range(2)]
        a_in = [sem(f"a_in{u}") for u in range(2)]
        prod_ready = sem("prod_ready")
        mask_done = sem("mask_done")
        mhi_ready = sem("mhi_ready")
        mlo_ready = sem("mlo_ready")
        cast_done = sem("cast_done")
        adj8_out = [sem(f"adj8_out{u}") for u in range(2)]
        adj8_in = [sem(f"adj8_in{u}") for u in range(2)]
        agg_done = sem("agg_done")
        gate_in = sem("gate_in")
        gate_out = sem("gate_out")
        coef_ready = sem("coef_ready")
        att_scaled = sem("att_scaled")
        z_ready = sem("z_ready")
        sig_ready = sem("sig_ready")
        var_ready = sem("var_ready")
        pow_ready = sem("pow_ready")
        x_ready = sem("x_ready")
        x_saved = sem("x_saved")
        transposed = sem("transposed")
        xT_ready = sem("xT_ready")
        projected = sem("projected")
        hb_ready = sem("hb_ready")
        yscale_ready = sem("yscale_ready")
        sum_read = sem("sum_read")
        hi_ready = sem("hi_ready")
        lo_ready = sem("lo_ready")
        result_out = [sem(f"result_out{u}") for u in range(2)]

        def wait(eng, s, value):
            if not (isinstance(value, int) and value <= 0):
                eng.wait_ge(s, value)

        def count(l, t):
            return l * NT + t + 1

        start_reg = {}

        def tile_of(eng, t):
            start = t * (P * NT * P)
            if not isinstance(t, int):
                if eng not in start_reg:
                    start_reg[eng] = eng.alloc_register("tile_start")
                eng.reg_mov(start_reg[eng], start)
                start = eng.snap(start_reg[eng])
            return scratch8[bass.ds(start, P * NT * P)].rearrange("(p f) -> p f", p=P)

        y_of = [ya, yb, ya, yb]

        block = ctx.enter_context(nc.Block())

        @block.sync
        def _(sp):
            sp.dma_start(wh[:], W_sa).then_inc(weights_in, 16)
            sp.dma_start(wg[:, :, 0:D], W_gcnb).then_inc(weights_in, 16)
            sp.dma_start(wg[:, :, D:D + 4], gate_cols).then_inc(weights_in, 16)
            sp.dma_start(asa_bc[:], a_sa.partition_broadcast(P)).then_inc(weights_in, 16)
            sp.dma_start(gate_bc[:], gate_bias.partition_broadcast(P)).then_inc(weights_in, 16)

            def load_adj32(t, u, p):
                wait(sp, cast_done, t - 1)
                wait(sp, mask_done, 2 * (t - 1))
                sp.dma_start(adj32[:, u, :], adjT[t]).then_inc(adj32_in[u], 16)

            def load_xT(t, b):
                wait(sp, h_projected, t - 3)
                sp.dma_start(xT[:, b], x_cols[t]).then_inc(xT_in[b], 16)

            def store_a(t):
                sp.wait_ge(ab_ready, t + 1)
                sp.dma_start(a_rows[t].rearrange("(p a) -> p a", a=1), abcols[:, t, 0:1]).then_inc(
                    a_out_first if isinstance(t, int) and t < 2 else a_out, 16)

            def load_a(t, u):
                wait(sp, prod_ready, 2 * (t - 1))
                sp.dma_start(a_bc[:, u, :], a_rows[t].partition_broadcast(P)).then_inc(a_in[u], 16)

            for t in range(4):
                load_xT(t, t)
            sp.dma_start(w2a_sb, W2a).then_inc(late_in, 16)
            sp.dma_start(w2b_sb, W2bT).then_inc(late_in, 16)
            sp.dma_start(b1col[:], b2a).then_inc(late_in, 16)
            sp.dma_start(bc_bc[:], b2b.partition_broadcast(P)).then_inc(late_in, 16)
            sp.dma_start(w1, W1g).then_inc(late_in, 16)
            sp.dma_start(w3, W3T).then_inc(late_in, 16)
            sp.dma_start(bg_bc[:], b_gcnb.partition_broadcast(P)).then_inc(late_in, 16)
            sp.dma_start(b1_bc[:], b1g.partition_broadcast(P)).then_inc(late_in, 16)
            sp.dma_start(b3_bc[:], b3.partition_broadcast(P)).then_inc(late_in, 16)

            def first(t, b):
                load_xT(t, b)
                store_a(t - 4)

            first(4, 0)
            first(5, 1)
            for q in range(2):
                for k in range(4):
                    first(6 + 4 * q + k, (6 + k) % 4)
                if q == 0:
                    sp.wait_ge(a_out_first, 16 * 2)
                    load_a(0, 0)
                    load_a(1, 1)
                else:
                    load_adj32(0, 0, 0)
            with sp.Fori(2, 5) as q:
                for k in range(4):
                    first(4 * q + 6 + k, (6 + k) % 4)
            load_adj32(1, 1, 0)
            sp.dma_start(xres[:], x_rows).then_inc(x_in, 16)
            for t in range(NT - 4, NT):
                store_a(t)
            sp.wait_ge(a_out, 16 * (NT - 2))

            def layer0(t, u, p, ahead=True):
                dst = tile_of(sp, t)
                sp.wait_ge(cast_done, t + 1)
                sp.dma_start(dst, adj8[:, u, :].bitcast(U8)).then_inc(adj8_out[u], 16)
                if ahead:
                    load_a(t + 2, u)
                    load_adj32(t + 2, u, p + 1)

            with sp.Fori(0, PAIRS - 1) as p:
                for u in range(2):
                    layer0(2 * p + u, u, p)
            for u in range(2):
                layer0(NT - 2 + u, u, PAIRS - 1, False)

            for u in range(2):
                sp.wait_ge(adj8_out[u], 16 * PAIRS)
            for l in range(1, 4):
                with sp.Fori(0, PAIRS) as p:
                    for u in range(2):
                        t = 2 * p + u
                        src = tile_of(sp, t)
                        sp.wait_ge(agg_done, count(l, t - 2))
                        sp.dma_start(adj8[:, u, :].bitcast(U8), src).then_inc(adj8_in[u], 16)

        @block.scalar
        def _(act):
            def first(t, u):
                act.wait_ge(small_ready, t + 1)
                nc.scalar.activation(abcols[:, t, :], small[:, u, 4:6], ACT.Exp,
                                     scale=-(1.0 - SLOPE))
                nc.scalar.activation(cols[:, t, 0:2], small[:, u, 4:6], ACT.Exp,
                                     scale=-SLOPE).then_inc(exps_ready, 1)
                nc.scalar.activation(ya[:, t, 0, 0:ONE], sum_ps[u][:, 0:ONE], ACT.Copy,
                                     scale=SY).then_inc(sums_hi, 1)
                act.wait_ge(ds_ready, t + 1)
                act.wait_ge(h_projected, t + 1)
                nc.scalar.activation(ym[:, t, 0, 0:D], att_ps[u][:, 0:D], ACT.Copy,
                                     scale=ds[:, u, :]).then_inc(h_hi, 1)

            act.wait_ge(late_in, 16 * 9)
            for w, n in ((w1, 0), (w3, 2)):
                nc.scalar.activation(w16[:, n, :, 0, :], w, ACT.Copy, scale=SW).then_inc(w16_hi, 1)

            def project_tiles(q0, q1):
                with act.Fori(q0, q1) as q:
                    for k in range(4):
                        first(4 * q + 2 + k, k % 2)

            def wait_for_cast(t, u, p):
                act.wait_ge(adj32_in[u], 16 * (p + 1))
                wait(act, agg_done, t - 1)
                wait(act, adj8_out[u], 16 * p)

            def cast(t, u):
                nc.scalar.copy(adj8[:, u, :], adj32[:, u, :], saturate=False).then_inc(cast_done, 1)

            def high_part(t, u, h):
                act.wait_ge(mask_done, 2 * t + h + 1)
                if h == 0:
                    wait(act, agg_done, t - 1)
                nc.scalar.copy(mhi[:, u, h * HALF * P:(h + 1) * HALF * P],
                               prod[:, h, :]).then_inc(mhi_ready, 1)

            def epilogue0(t, v):
                act.wait_ge(gate_in, t + 1)
                nc.scalar.activation(gates[:, v, :], gates[:, v, :], ACT.Sigmoid).then_inc(gate_out, 1)
                act.wait_ge(coef_ready, t + 1)
                nc.scalar.activation(t3[:], att_ps[v][:, 0:D], ACT.Copy,
                                     scale=coef[:, v, :]).then_inc(att_scaled, 1)
                act.wait_ge(z_ready, t + 1)
                nc.scalar.activation(sg[:], z[:], ACT.Sigmoid).then_inc(sig_ready, 1)

            def xT_high(l, t, v):
                act.wait_ge(transposed, count(l, t))
                nc.scalar.activation(xTh[:, v], tr_ps[:], ACT.Copy, scale=SX).then_inc(xT_hi, 1)

            def rows(l, t, v):
                act.wait_ge(projected, count(l, t))
                dst = y_of[l + 1][:, t, 0, 0:D]
                if l < 2:
                    act.wait_ge(yscale_ready, count(l, t))
                if l == 0:
                    nc.scalar.activation(dst, pj_ps[:, 0:D], ACT.Copy,
                                         scale=yscale[:, v, :]).then_inc(hi_ready, 1)
                elif l == 1:
                    act.wait_ge(hb_ready, t + 1)
                    nc.scalar.activation(dst, hb, ACT.Copy, scale=yscale[:, v, :]).then_inc(hi_ready, 1)
                else:
                    act.wait_ge(hb_ready, NT + t + 1)
                    nc.scalar.activation(dst, hb, ACT.Copy, scale=SY).then_inc(hi_ready, 1)

            def window0(t, u, p, ahead=True):
                v = 1 - u
                has_prev = not (isinstance(t, int) and t == 0)
                if ahead:
                    wait_for_cast(t + 1, v, p + u)
                if has_prev:
                    epilogue0(t - 1, v)
                if ahead:
                    high_part(t + 1, v, 0)
                    high_part(t + 1, v, 1)
                if has_prev:
                    xT_high(0, t - 1, v)
                if ahead:
                    cast(t + 1, v)
                if has_prev:
                    rows(0, t - 1, v)

            first(0, 0)
            first(1, 1)
            project_tiles(0, MIDDLE)
            wait_for_cast(0, 0, 0)
            cast(0, 0)
            project_tiles(MIDDLE, 6)

            act.wait_ge(comb_done, 1)
            for c in range(KC):
                nc.scalar.activation(w16[:, 1, c, 0, :], sum_ps[c][:, 0:D], ACT.Copy,
                                     scale=SW).then_inc(w16_hi, 1)

            high_part(0, 0, 0)
            high_part(0, 0, 1)
            for u in range(2):
                window0(u, u, 0)
            with act.Fori(1, PAIRS - 1) as p:
                for u in range(2):
                    window0(2 * p + u, u, p)
            for u in range(2):
                window0(NT - 2 + u, u, PAIRS - 1, ahead=(u == 0))

            epilogue0(NT - 1, 1)
            xT_high(0, NT - 1, 1)
            rows(0, NT - 1, 1)
            for l in range(1, 3):
                with act.Fori(0, PAIRS) as p:
                    for v in range(2):
                        xT_high(l, 2 * p + v, v)
                        rows(l, 2 * p + v, v)

        @block.gpsimd
        def _(pool):
            nc.gpsimd.memset(minus_half[:], -0.5).then_inc(consts_made, 1)
            nc.gpsimd.memset(ident[:], 0.0).then_inc(ident_made, 1)
            pool.wait_ge(ident_made, 1)
            nc.gpsimd.affine_select(out=ident[:], in_=ident[:], compare_op=ALU.not_equal, fill=1.0, base=0,
                                    pattern=[[-1, P]], channel_multiplier=1).then_inc(ident_made, 1)
            pool.wait_ge(ident_made, 2)
            nc.gpsimd.tensor_copy(ident16[:], ident[:]).then_inc(ident_made, 1)
            nc.gpsimd.memset(ya[:, :, 0, ONE:ONE + 1], 1.0).then_inc(ident_made, 1)
            pool.wait_ge(consts_made, 1)

            def product(t, u, h, p):
                if h == 0:
                    pool.wait_ge(a_in[u], 16 * (p + 1))
                wait(pool, mlo_ready, 2 * (t - 1) + h + 1)
                wait(pool, mhi_ready, 2 * (t - 1) + h + 1)
                b = abcols[:, h * HALF:(h + 1) * HALF, 1:2].broadcast_to([P, HALF, P])
                a = a_bc[:, u:u + 1, :].broadcast_to([P, HALF, P])
                nc.gpsimd.tensor_tensor(prod[:, h, :].rearrange("p (j i) -> p j i", i=P), a, b,
                                        ALU.mult).then_inc(prod_ready, 1)

            def power(l, t, v):
                n = 3 if l == 0 else 1
                pool.wait_ge(var_ready, count(l, t))
                nc.gpsimd.tensor_tensor(pow_out[:, v, 0:n], pow_in[:, v, 0:n], minus_half[:, 0:n],
                                        ALU.pow).then_inc(pow_ready, 1)

            def save_x(l, t, v):
                pool.wait_ge(x_ready, count(l, t))
                nc.gpsimd.tensor_copy(xres[:, t, :], xn[:, v, :]).then_inc(x_saved, 1)

            def window0(t, u, p, ahead=True):
                v = 1 - u
                has_prev = not (isinstance(t, int) and t == 0)
                if has_prev:
                    power(0, t - 1, v)
                if ahead:
                    product(t + 2, u, 0, p + 1)
                if has_prev:
                    save_x(0, t - 1, v)
                if ahead:
                    product(t + 2, u, 1, p + 1)

            pool.wait_ge(ab_ready, HALF)
            product(0, 0, 0, 0)
            pool.wait_ge(ab_ready, NT)
            product(0, 0, 1, 0)
            for h in range(2):
                product(1, 1, h, 0)
            for u in range(2):
                window0(u, u, 0)
            with pool.Fori(1, PAIRS - 1) as p:
                for u in range(2):
                    window0(2 * p + u, u, p)
            for u in range(2):
                window0(NT - 2 + u, u, PAIRS - 1, False)
            power(0, NT - 1, 1)
            save_x(0, NT - 1, 1)
            for l in range(1, 4):
                with pool.Fori(0, PAIRS) as p:
                    for v in range(2):
                        t = 2 * p + v
                        power(l, t, v)
                        if l < 3:
                            save_x(l, t, v)
                        else:
                            pool.wait_ge(x_ready, count(l, t))
                            pool.dma_start(out[t], xn[:, v, :]).then_inc(result_out[v], 16)
            for v in range(2):
                pool.wait_ge(result_out[v], 16 * PAIRS)

        @block.vector
        def _(dve):
            done = [0]

            def link(ins):
                done[0] = done[0] + 1
                ins.then_inc(vec, 1)

            def linked():
                dve.wait_ge(vec, done[0])

            dve.wait_ge(weights_in, 16 * 5)
            for c in range(KC):
                for side in range(2):
                    nc.vector.tensor_tensor_reduce(
                        out=(t1, t3, z, sg)[2 * c + side][:], in0=wh[:, c, :], in1=asa_bc[:, side, :], scale=1.0, scalar=0.0,
                        op0=ALU.mult, op1=ALU.add,
                        accum_out=wg[:, c, D + 4 + side:D + 5 + side]).then_inc(proj_cols_made, 1)

            def h_low(t, u):
                dve.wait_ge(h_hi, t + 1)
                nc.vector.scalar_tensor_tensor(ym[:, t, 1, 0:D], att_ps[u][:, 0:D], ds[:, u, :], ym[:, t, 0, 0:D],
                                               ALU.mult, ALU.subtract).then_inc(h_lo, 1)

            def first(t, u):
                done[0] = t
                dve.wait_ge(sums_projected, t + 1)
                nc.vector.tensor_copy(small[:, u, :], sum_ps[u][:, D:WG]).then_inc(small_ready, 1)
                if not (isinstance(t, int) and t == 0):
                    h_low(t - 1, 1 - u)
                dve.wait_ge(exps_ready, t + 1)
                nc.vector.tensor_scalar(ds[:, u, :], cols[:, t, 1:2], SY, None, ALU.mult).then_inc(ds_ready, 1)
                nc.vector.tensor_scalar(abcols[:, t, :], abcols[:, t, :], SAB, None, ALU.mult).then_inc(ab_ready, 1)
                nc.vector.tensor_tensor(cols[:, t, 2:4], small[:, u, 2:4], gate_bc[:], ALU.add)
                dve.wait_ge(ds_ready, t + 1)
                link(nc.vector.tensor_copy(ym[:, t, 0, D:WM], ds[:, u, :]))
                dve.wait_ge(sums_hi, t + 1)
                nc.vector.scalar_tensor_tensor(ya[:, t, 1, 0:ONE], sum_ps[u][:, 0:ONE], SY, ya[:, t, 0, 0:ONE],
                                               ALU.mult, ALU.subtract).then_inc(sums_lo, 1)
                linked()
                nc.vector.tensor_tensor(ym[:, t, 1, D:WM], ds[:, u, :], ym[:, t, 0, D:WM], ALU.subtract)

            for u in range(2):
                first(u, u)
            with dve.Fori(0, 6) as q:
                for k in range(4):
                    first(4 * q + 2 + k, k % 2)
            h_low(NT - 1, 1)
            done[0] = NT

            dve.wait_ge(late_in, 16 * 9)
            link(nc.vector.memset(b1rep[:], 1.0))
            linked()
            nc.vector.tensor_scalar(b1rep[:], b1rep[:], b1col[:], None, ALU.mult).then_inc(comb_ready, 1)
            for i, (w, n) in enumerate(((w1, 0), (w3, 2))):
                dve.wait_ge(w16_hi, i + 1)
                for c in range(KC):
                    nc.vector.scalar_tensor_tensor(w16[:, n, c, 1, :], w[:, c, :], SW, w16[:, n, c, 0, :],
                                                   ALU.mult, ALU.subtract).then_inc(w16_ready, 1)
            dve.wait_ge(comb_done, 1)
            nc.vector.tensor_tensor(bc_bc[:], att_ps[0][:, 0:D], bc_bc[:], ALU.add).then_inc(comb_saved, 1)
            for c in range(KC):
                dve.wait_ge(w16_hi, 3 + c)
                nc.vector.scalar_tensor_tensor(w16[:, 1, c, 1, :], sum_ps[c][:, 0:D], SW, w16[:, 1, c, 0, :],
                                               ALU.mult, ALU.subtract).then_inc(w16_ready, 1)
            base0 = NT + 1

            def mask(t, u, h, p):
                dve.wait_ge(prod_ready, 2 * t + h + 1)
                if h == 0:
                    dve.wait_ge(adj32_in[u], 16 * (p + 1))
                nc.vector.scalar_tensor_tensor(prod[:, h, :], prod[:, h, :], SM,
                                               adj32[:, u, h * HALF * P:(h + 1) * HALF * P],
                                               ALU.min, ALU.mult).then_inc(mask_done, 1)

            def low_part(t, u, h):
                part = slice(h * HALF * P, (h + 1) * HALF * P)
                dve.wait_ge(mhi_ready, 2 * t + h + 1)
                nc.vector.tensor_tensor(mlo[:, u, part], prod[:, h, :], mhi[:, u, part],
                                        ALU.subtract).then_inc(mlo_ready, 1)

            def variance(v):
                link(nc.vector.bn_stats(stats[:, 0:6], xs[:, v, :]))
                linked()
                nc.vector.tensor_copy(stats[:, 6:7], stats[:, 0:1])
                link(nc.vector.bn_aggr(mean_var[:, v, :], stats[:, 0:6]))
                linked()
                nc.vector.tensor_scalar(pow_in[:, v, 0:1], mean_var[:, v, 1:2], EPS_LN, None,
                                        ALU.add).then_inc(var_ready, 1)

            def normalize(l, t, v):
                dve.wait_ge(pow_ready, count(l, t))
                if l in (1, 2):
                    wait(dve, transposed, count(l, t - 2))
                    wait(dve, x_saved, count(l, t - 2))
                nc.vector.tensor_scalar(xn[:, v, :], xs[:, v, :], mean_var[:, v, 0:1], pow_out[:, v, 0:1],
                                        ALU.subtract, ALU.mult).then_inc(x_ready, 1)

            LINKS0 = 8

            def epilogue0(t, v, p, ahead):
                done[0] = base0 + LINKS0 * t
                T, M = sum_ps[v], att_ps[v]
                link(nc.vector.tensor_copy(own[:, v, 0:4], cols[:, t, 0:4]))
                dve.wait_ge(agg_done, t + 1)
                linked()
                nc.vector.scalar_tensor_tensor(gates[:, v, :], T[:, GA:GA + 2], 1.0 / SY, own[:, v, 2:4],
                                               ALU.mult, ALU.add).then_inc(gate_in, 1)
                link(nc.vector.tensor_scalar(den[:, 0:1], M[:, D:WM], own[:, v, 0:1], EPS_ATT * SM * SY,
                                             ALU.mult, ALU.add))
                linked()
                link(nc.vector.reciprocal(den[:, 1:2], den[:, 0:1]))
                link(nc.vector.scalar_tensor_tensor(t1[:], T[:, 0:D], 1.0 / SY, bg_bc[:], ALU.mult, ALU.add))
                dve.wait_ge(gate_out, t + 1)
                linked()
                nc.vector.scalar_tensor_tensor(coef[:, v, :], den[:, 1:2], own[:, v, 0:1], gates[:, v, 0:1],
                                               ALU.mult, ALU.mult).then_inc(coef_ready, 1)
                nc.vector.tensor_scalar(pow_in[:, v, 1:2], T[:, ONE:WT], TINY, None, ALU.max)
                nc.vector.tensor_scalar(pow_in[:, v, 2:3], T[:, ONE:WT], 1.0, TINY, ALU.add, ALU.max)
                link(nc.vector.tensor_scalar(den[:, 2:3], T[:, ONE:WT], 0.0, None, ALU.is_gt))
                if ahead:
                    mask(t + 2, v, 0, p)
                dve.wait_ge(att_scaled, t + 1)
                nc.vector.scalar_tensor_tensor(z[:], t1[:], gates[:, v, 1:2], t3[:],
                                               ALU.mult, ALU.add).then_inc(z_ready, 1)
                if ahead:
                    mask(t + 2, v, 1, p)
                dve.wait_ge(sig_ready, t + 1)
                if isinstance(t, int) and t == 0:
                    dve.wait_ge(x_in, 16)
                link(nc.vector.tensor_tensor(xs[:, v, :], sg[:], xres[:, t, :], ALU.add))
                linked()
                variance(v)
                if ahead:
                    low_part(t + 2, v, 0)
                normalize(0, t, v)
                nc.vector.tensor_tensor(cols[:, t, 4:5], pow_out[:, v, 1:2], den[:, 2:3], ALU.mult)
                nc.vector.tensor_copy(cols[:, t, 5:6], pow_out[:, v, 2:3])
                nc.vector.scalar_tensor_tensor(yscale[:, v, :], pow_out[:, v, 1:2], SY / (SX * SW), den[:, 2:3],
                                               ALU.mult, ALU.mult).then_inc(yscale_ready, 1)

            def xT_low(l, t, v):
                dve.wait_ge(xT_hi, count(l, t))
                nc.vector.scalar_tensor_tensor(xTl[:, v], tr_ps[:], SX, xTh[:, v],
                                               ALU.mult, ALU.subtract).then_inc(xT_ready, 1)

            def biased(l, t):
                dve.wait_ge(projected, count(l, t))
                nc.vector.scalar_tensor_tensor(hb, pj_ps[:, 0:D], 1.0 / (SX * SW), (bc_bc if l == 1 else b3_bc)[:],
                                               ALU.mult, ALU.add).then_inc(hb_ready, 1)

            def rows(l, t, v):
                y = y_of[l + 1]
                dve.wait_ge(projected, count(l, t))
                if l < 2:
                    dve.wait_ge(yscale_ready, count(l, t))
                if l == 0:
                    dve.wait_ge(hi_ready, count(l, t))
                    nc.vector.scalar_tensor_tensor(y[:, t, 1, 0:D], pj_ps[:, 0:D], yscale[:, v, :],
                                                   y[:, t, 0, 0:D], ALU.mult, ALU.subtract).then_inc(lo_ready, 1)
                else:
                    dve.wait_ge(hi_ready, count(l, t))
                    nc.vector.scalar_tensor_tensor(y[:, t, 1, 0:D], hb, yscale[:, v, :] if l == 1 else SY,
                                                   y[:, t, 0, 0:D], ALU.mult, ALU.subtract).then_inc(lo_ready, 1)

            LINKS, LINKS3 = 5, 3

            def epilogue(l, t, v):
                done[0] = base0 + LINKS0 * NT + LINKS * (NT * (l - 1) + t)
                A = sum_ps[v]
                link(nc.vector.tensor_copy(own[:, v, 4:6], cols[:, t, 4:6]))
                linked()
                if l == 1:
                    link(nc.vector.tensor_scalar(escale[:, v, :], own[:, v, 4:5], 1.0 / SY, None, ALU.mult))
                    nc.vector.tensor_scalar(yscale[:, v, :], own[:, v, 5:6], SY, None,
                                            ALU.mult).then_inc(yscale_ready, 1)
                else:
                    link(nc.vector.tensor_scalar(escale[:, v, :], own[:, v, 5:6], 1.0 / SY, None, ALU.mult))
                linked()
                dve.wait_ge(agg_done, count(l, t))
                wait(dve, x_saved, count(l - 1, t))
                if l == 1:
                    nc.vector.scalar_tensor_tensor(t1[:], A[:, 0:D], escale[:, v, :], b1_bc[:],
                                                   ALU.mult, ALU.add).then_inc(sum_read, 1)
                    dve.wait_ge(sum_read, t + 1)
                    link(nc.vector.scalar_tensor_tensor(xs[:, v, :], t1[:], 0.0, xres[:, t, :], ALU.max, ALU.add))
                else:
                    link(nc.vector.scalar_tensor_tensor(xs[:, v, :], A[:, 0:D], escale[:, v, :],
                                                        xres[:, t, :], ALU.mult, ALU.add))
                linked()
                variance(v)
                normalize(l, t, v)

            def epilogue3(t, v, p):
                done[0] = base0 + LINKS0 * NT + LINKS * NT * 2 + LINKS3 * t
                dve.wait_ge(agg_done, count(3, t))
                dve.wait_ge(x_ready, count(3, t - 2))
                dve.wait_ge(x_saved, count(2, t))
                link(nc.vector.scalar_tensor_tensor(xs[:, v, :], sum_ps[v][:, 0:D], 1.0 / SY, xres[:, t, :],
                                                    ALU.mult, ALU.add))
                linked()
                wait(dve, result_out[v], 16 * p)
                if isinstance(t, int):
                    dve.wait_ge(transposed, count(2, NT - 1))
                    dve.wait_ge(x_saved, count(2, NT - 1))
                variance(v)
                normalize(3, t, v)

            def window0(t, u, p, ahead=True):
                v = 1 - u
                has_prev = not (isinstance(t, int) and t == 0)
                if has_prev:
                    epilogue0(t - 1, v, p + u, ahead)
                else:
                    for h in range(2):
                        mask(1, 1, h, 0)
                    low_part(1, 1, 0)
                if ahead:
                    low_part(t + 1, v, 1)
                if has_prev:
                    xT_low(0, t - 1, v)
                    rows(0, t - 1, v)

            for h in range(2):
                mask(0, 0, h, 0)
            for h in range(2):
                low_part(0, 0, h)
            for u in range(2):
                window0(u, u, 0)
            with dve.Fori(1, PAIRS - 1) as p:
                for u in range(2):
                    window0(2 * p + u, u, p)
            for u in range(2):
                window0(NT - 2 + u, u, PAIRS - 1, ahead=(u == 0))
            epilogue0(NT - 1, 1, PAIRS, False)
            xT_low(0, NT - 1, 1)
            rows(0, NT - 1, 1)

            def turn(l, p, first=False):
                for v in range(2):
                    t = 2 * p + v
                    if l < 3 and not (first and v == 0):
                        xT_low(l, t - 1, 1 - v)
                        biased(l, t - 1)
                    if l < 3:
                        epilogue(l, t, v)
                    else:
                        epilogue3(t, v, p)
                    if l < 3 and not (first and v == 0):
                        rows(l, t - 1, 1 - v)

            for l in range(1, 4):
                turn(l, 0, True)
                with dve.Fori(1, PAIRS) as p:
                    turn(l, p)
                if l < 3:
                    xT_low(l, NT - 1, 1)
                    biased(l, NT - 1)
                    rows(l, NT - 1, 1)

        @block.tensor
        def _(pe):
            pe.wait_ge(weights_in, 16 * 5)
            pe.wait_ge(proj_cols_made, 2 * KC)

            def first(t, u, b, turn):
                pe.wait_ge(xT_in[b], 16 * (turn + 1))
                wait(pe, sums_lo, t - 1)
                for c in range(KC):
                    last = nc.tensor.matmul(sum_ps[u][:, 0:WG], xT[:, b, c, :], wg[:, c, :],
                                            start=(c == 0), stop=(c == KC - 1))
                last.then_inc(sums_projected, 1)
                wait(pe, h_lo, t - 1)
                for c in range(KC):
                    last = nc.tensor.matmul(att_ps[u][:, 0:D], xT[:, b, c, :], wh[:, c, :],
                                            start=(c == 0), stop=(c == KC - 1))
                last.then_inc(h_projected, 1)

            for u in range(2):
                first(u, u, u, 0)
            with pe.Fori(0, 6) as q:
                for k in range(4):
                    first(4 * q + 2 + k, k % 2, (2 + k) % 4, q + (2 + k) // 4)

            pe.wait_ge(comb_ready, 1)
            pe.wait_ge(late_in, 16 * 9)
            pe.wait_ge(sums_lo, NT)
            pe.wait_ge(h_lo, NT)
            for c in range(KC):
                nc.tensor.matmul(sum_ps[c][:, 0:D], w2a_sb[:, c * P:(c + 1) * P], w2b_sb, start=True, stop=True)
            nc.tensor.matmul(att_ps[0][:, 0:D], b1rep[:], w2b_sb, start=True, stop=True).then_inc(comb_done, 1)
            pe.wait_ge(comb_saved, 1)
            pe.wait_ge(w16_ready, 3 * KC)
            pe.wait_ge(ident_made, 4)

            def transpose(l, t, v):
                pe.wait_ge(x_ready, count(l, t))
                wait(pe, xT_ready, count(l, t) - 1)
                for c in range(KC):
                    last = nc.tensor.transpose(tr_ps[:, c, :], xn[:, v, c * P:(c + 1) * P], ident[:])
                last.then_inc(transposed, 1)

            def project(l, t, v):
                pe.wait_ge(xT_ready, count(l, t))
                wait(pe, lo_ready, count(l, t) - 1)
                terms = [(x, c, part) for c in range(KC) for x, part in ((xTh, 0), (xTh, 1), (xTl, 0))]
                for n, (x, c, part) in enumerate(terms):
                    last = nc.tensor.matmul(pj_ps[:, 0:D], x[:, v, c, :], w16[:, l, c, part, :],
                                            start=(n == 0), stop=(n == len(terms) - 1))
                last.then_inc(projected, 1)

            def window0(t, u):
                v = 1 - u
                has_prev = not (isinstance(t, int) and t == 0)
                wait(pe, x_ready, t - 1)
                pe.wait_ge(cast_done, t + 1)
                def attention(last_part):
                    for j in range(NT):
                        if j % HALF == 0:
                            pe.wait_ge(mlo_ready, 2 * t + j // HALF + 1)
                        hi, lo = mhi[:, u, j * P:(j + 1) * P], mlo[:, u, j * P:(j + 1) * P]
                        nc.tensor.matmul(att_ps[u][:, 0:WM], hi, ym[:, j, 0, 0:WM], start=(j == 0), stop=False)
                        nc.tensor.matmul(att_ps[u][:, 0:WM], hi, ym[:, j, 1, 0:WM], start=False, stop=False)
                        last = nc.tensor.matmul(att_ps[u][:, 0:WM], lo, ym[:, j, 0, 0:WM],
                                                start=False, stop=(j == NT - 1))
                    if last_part:
                        last.then_inc(agg_done, 1)

                def neighbours(last_part):
                    for j in range(NT):
                        if has_prev and j == TRANSPOSE0_AT:
                            transpose(0, t - 1, v)
                        if has_prev and j == PROJECT0_AT:
                            project(0, t - 1, v)
                        w = adj8[:, u, j * P:(j + 1) * P]
                        nc.tensor.matmul(sum_ps[u][:, 0:WT], w, ya[:, j, 0, 0:WT], start=(j == 0), stop=False)
                        last = nc.tensor.matmul(sum_ps[u][:, 0:ONE], w, ya[:, j, 1, 0:ONE], start=False,
                                                stop=(j == NT - 1))
                    if last_part:
                        last.then_inc(agg_done, 1)

                if has_prev:
                    attention(False)
                    neighbours(True)
                else:
                    neighbours(False)
                    attention(True)

            for u in range(2):
                window0(u, u)
            with pe.Fori(1, PAIRS) as p:
                for u in range(2):
                    window0(2 * p + u, u)

            def window(l, t, u, p):
                v = 1 - u
                y = y_of[l]
                starts = isinstance(t, int) and t == 0
                pe.wait_ge(x_ready, count(l, t - 2))
                pe.wait_ge(adj8_in[u], 16 * (PAIRS * (l - 1) + p + 1))
                if l == 2:
                    if starts:
                        pe.wait_ge(lo_ready, count(1, 0))
                    nc.tensor.matmul(sum_ps[u][:, 0:D], ident16[:], y[:, t, 0, 0:D], start=True, stop=False)
                    nc.tensor.matmul(sum_ps[u][:, 0:D], ident16[:], y[:, t, 1, 0:D], start=False, stop=False)
                else:
                    nc.tensor.matmul(idle_ps[:, 0:1], ident16[:], ident16[:, 0:1], start=True, stop=True)
                for j in range(NT):
                    if j == TRANSPOSE_AT:
                        if starts:
                            transpose(l - 1, NT - 1, v)
                        elif l < 3:
                            transpose(l, t - 1, v)
                    if j == PROJECT_AT:
                        if starts:
                            project(l - 1, NT - 1, v)
                        elif l < 3:
                            project(l, t - 1, v)
                    if starts:
                        pe.wait_ge(lo_ready, count(l - 1, j))
                    w = adj8[:, u, j * P:(j + 1) * P]
                    nc.tensor.matmul(sum_ps[u][:, 0:D], w, y[:, j, 0, 0:D], start=(l != 2 and j == 0), stop=False)
                    last = nc.tensor.matmul(sum_ps[u][:, 0:D], w, y[:, j, 1, 0:D], start=False, stop=(j == NT - 1))
                last.then_inc(agg_done, 1)

            for l in range(1, 4):
                for u in range(2):
                    window(l, u, u, 0)
                with pe.Fori(1, PAIRS) as p:
                    for u in range(2):
                        window(l, 2 * p + u, u, p)




def kernel(**inputs):
    import numpy as np
    import concourse.bacc as bacc
    from concourse.bass_utils import run_bass_kernel_spmd as run

    v = {k: np.ascontiguousarray(a) for k, a in inputs.items()}
    pad = NT * P - N

    adjT = np.pad(v["adj"], ((0, pad), (0, pad))).reshape(NT, P, NT, P)
    xp = np.pad(v["x"], ((0, pad), (0, 0))).reshape(NT, P, D)
    chunks = lambda w: w.reshape(KC, P, -1).transpose(1, 0, 2)
    wa, wb = v["L0_gnn_Wa"].reshape(2, D), v["L0_gnn_Wb"].reshape(2, D)
    arrays = {
        "adjT": adjT.transpose(0, 3, 2, 1).reshape(NT, P, NT * P),
        "x_rows": xp.transpose(1, 0, 2),
        "x_cols": xp.reshape(NT, P, KC, P).transpose(0, 3, 2, 1),
        "W_sa": chunks(v["L0_gnn_W_sa"]),
        "a_sa": v["L0_gnn_a_sa"].reshape(2, D),
        "W_gcnb": chunks(v["L0_gnn_W_gcnb"]),
        "b_gcnb": v["L0_gnn_b_gcnb"],
        "gate_cols": chunks(np.stack([wa[0], wb[0], wa[1], wb[1]], axis=1)),
        "gate_bias": np.concatenate([v["L0_gnn_ba"], v["L0_gnn_bb"]]),
        "W1g": chunks(v["L1_gnn_W"]),
        "b1g": v["L1_gnn_b"],
        "W2a": v["L2_gnn_W1"],
        "b2a": v["L2_gnn_b1"].reshape(P, 1),
        "W2bT": v["L2_gnn_W2"].T,
        "b2b": v["L2_gnn_b2"],
        "W3T": chunks(v["L3_gnn_W"].T),
        "b3": v["L3_gnn_b"],
    }
    nc = bacc.Bacc("TRN2", target_bir_lowering=False, num_devices=1)
    arrays = {k: np.ascontiguousarray(a) for k, a in arrays.items()}
    aps = [nc.dram_tensor(k, a.shape, mybir.dt.from_np(a.dtype), kind="ExternalInput").ap()
           for k, a in arrays.items()]
    out = nc.dram_tensor("out", (NT, P, D), F32, kind="ExternalOutput").ap()
    resnorm_gnn_kernel(nc, *aps, out)
    r = run(nc, [arrays], core_ids=[0])
    return r.results[0]["out"].reshape(NT * P, D)[:N]
```

```python
from contextlib import ExitStack

import concourse.bass as bass
from concourse import mybir

ALU = mybir.AluOpType
ACT = mybir.ActivationFunctionType
F32 = mybir.dt.float32
F16 = mybir.dt.float16
F8 = mybir.dt.float8e4
U8 = mybir.dt.uint8

P = 128
N = 3327
NT = -(-N // P)
PAIRS = NT // 2
D = 256
KC = D // P
HALF = NT // 2
TURNS = (NT - 2) // 4
WEIGHTS_TURN, COMB_TURN, MASK_TURN = 1, 2, 4
EPS_LN = 1e-5
EPS_ATT = 1e-5
SLOPE = 0.01
SY = 256.0
SX = 256.0
SW = 256.0
SAB = 32.0
SM = SAB * SAB
TINY = 1e-30

TRANSPOSE0_AT, PROJECT0_AT = 3, 14
SECOND_TRANSPOSE_AT, SECOND_PROJECT_AT = 15, 23
TRANSPOSE_AT, PROJECT_AT = 21, 2
START_TRANSPOSE_AT = (NT - 1, 18, 18)
START_PROJECT_AT = (NT + 5, 24, 24)
BETWEEN = (13, 7, 7)

GA = D
ONE = D + 2
WT = D + 3
WTP = D + 4
WM = D + 1
WMP = D + 2
SMALL = 6
WG = D + SMALL


def resnorm_gnn_kernel(nc, adjT, x_rows, x_cols, W_sa, a_sa, W_gcnb, b_gcnb, gate_cols, gate_bias,
                       W1g, b1g, W2a, b2a, W2bT, b2b, W3T, b3, out):
    scratch8 = nc.dram_tensor("adj8", [NT * P * NT * P], U8, kind="Internal").ap()
    a_rows = nc.dram_tensor("a_rows", [NT, P], F32, kind="Internal").ap()

    with ExitStack() as ctx:
        def sb(name, shape, dt):
            return ctx.enter_context(nc.sbuf_tensor(name, shape, dt))

        def ps(name, shape):
            return ctx.enter_context(nc.psum_tensor(name, shape, F32))

        def sem(name):
            return ctx.enter_context(nc.semaphore(name))

        ya = sb("ya", [P, NT, 2, WTP], F16)
        yb = sb("yb", [P, NT, 2, D], F16)
        ym = sb("ym", [P, NT, 2, WMP], F16)
        xres = sb("xres", [P, NT, D], F32)
        cols = sb("cols", [P, NT, 6], F32)
        abcols = sb("abcols", [P, NT, 2], F32)
        adj32 = sb("adj32", [P, 2, NT * P], F32)
        adj8 = sb("adj8_sb", [P, 2, NT * P], F8)
        prod = sb("prod", [P, 2, HALF * P], F32)
        mhi = sb("mhi", [P, 2, NT * P], F16)
        mlo = sb("mlo", [P, 2, NT * P], F16)
        a_bc = sb("a_bc", [P, 2, P], F32)

        wh = sb("wh", [P, KC, D], F32)
        wg = sb("wg", [P, KC, WG], F32)
        w16 = sb("w16", [P, 3, KC, 2, D], F16)
        staged = mlo[:, 1, :].bitcast(F32)
        w1 = staged[:, 0:KC * D].rearrange("p (c n) -> p c n", c=KC)
        w3 = staged[:, KC * D:2 * KC * D].rearrange("p (c n) -> p c n", c=KC)
        w2a_sb = staged[:, 2 * KC * D:2 * KC * D + D]
        w2b_sb = staged[:, 2 * KC * D + D:2 * KC * D + 2 * D]
        b1col = sb("b1col", [P, 1], F32)
        b1rep = sb("b1rep", [P, P], F32)
        asa_bc = sb("asa_bc", [P, 2, D], F32)
        bg_bc = sb("bg_bc", [P, D], F32)
        b1_bc = sb("b1_bc", [P, D], F32)
        bc_bc = sb("bc_bc", [P, D], F32)
        b3_bc = sb("b3_bc", [P, D], F32)
        gate_bc = sb("gate_bc", [P, 2], F32)
        ident = sb("ident", [P, P], F32)
        ident16 = sb("ident16", [P, P], F16)
        minus_half = sb("minus_half", [P, 3], F32)

        xT = mhi[:, 0, 0:4 * KC * P * 2].bitcast(F32).rearrange("p (b c i) -> p b c i", b=4, c=KC)
        xTh = sb("xTh", [P, 2, KC, P], F16)
        xTl = sb("xTl", [P, 2, KC, P], F16)
        xn = sb("xn", [P, 2, D], F32)
        small = sb("small", [P, 2, SMALL], F32)
        ds = sb("ds", [P, 2, 1], F32)
        own = sb("own", [P, 2, 6], F32)
        den = sb("den", [P, 3], F32)
        gates = sb("gates", [P, 2, 2], F32)
        coef = sb("coef", [P, 2, 1], F32)
        escale = sb("escale", [P, 2, 1], F32)
        yscale = sb("yscale", [P, 2, 1], F32)
        t1 = sb("t1", [P, D], F32)
        t3 = sb("t3", [P, D], F32)
        z = sb("z", [P, D], F32)
        sg = sb("sg", [P, D], F32)
        xs = sb("xs", [P, 2, D], F32)
        hb = asa_bc[:, 0, :]
        stats = sb("stats", [P, 7], F32)
        mean_var = sb("mean_var", [P, 2, 2], F32)
        pow_in = sb("pow_in", [P, 2, 3], F32)
        pow_out = sb("pow_out", [P, 2, 3], F32)

        sum_ps = [ps(f"sum_ps{u}", [P, 512]) for u in range(2)]
        att_ps = [ps(f"att_ps{u}", [P, 512]) for u in range(2)]
        tr_ps = ps("tr_ps", [P, KC, P])
        pj_ps = ps("pj_ps", [P, 512])
        idle_ps = ps("idle_ps", [P, 512])
        comb_ps = [pj_ps[:, 0:D], idle_ps[:, 0:D]]
        b1w2_ps = tr_ps[:].rearrange("p c i -> p (c i)")

        wh_in = sem("wh_in")
        wg_in = sem("wg_in")
        asa_in = sem("asa_in")
        late_in = sem("late_in")
        x_in = sem("x_in")
        ident_made = sem("ident_made")
        consts_made = sem("consts_made")
        proj_cols_made = sem("proj_cols_made")
        ones_made = sem("ones_made")
        comb_ready = sem("comb_ready")
        comb_done = sem("comb_done")
        comb_saved = sem("comb_saved")
        xT_in = [sem(f"xT_in{b}") for b in range(4)]
        sums_projected = sem("sums_projected")
        h_projected = sem("h_projected")
        small_ready = sem("small_ready")
        exps_ready = sem("exps_ready")
        ab_ready = sem("ab_ready")
        ds_ready = sem("ds_ready")
        sums_hi = sem("sums_hi")
        sums_lo = sem("sums_lo")
        h_hi = sem("h_hi")
        h_lo = sem("h_lo")
        w16_hi = sem("w16_hi")
        w16_ready = sem("w16_ready")
        xT_hi = sem("xT_hi")
        a_out = sem("a_out")
        a_out_first = sem("a_out_first")
        vec = sem("vec")
        adj32_in = [sem(f"adj32_in{u}") for u in range(2)]
        a_in = [sem(f"a_in{u}") for u in range(2)]
        prod_ready = sem("prod_ready")
        mask_done = sem("mask_done")
        mhi_ready = sem("mhi_ready")
        mlo_ready = sem("mlo_ready")
        cast_done = sem("cast_done")
        adj8_out = [sem(f"adj8_out{u}") for u in range(2)]
        adj8_in = [sem(f"adj8_in{u}") for u in range(2)]
        agg_done = sem("agg_done")
        gate_in = sem("gate_in")
        gate_out = sem("gate_out")
        coef_ready = sem("coef_ready")
        att_scaled = sem("att_scaled")
        z_ready = sem("z_ready")
        sig_ready = sem("sig_ready")
        var_ready = sem("var_ready")
        pow_ready = sem("pow_ready")
        x_ready = sem("x_ready")
        x_saved = sem("x_saved")
        transposed = sem("transposed")
        xT_ready = sem("xT_ready")
        projected = sem("projected")
        hb_ready = sem("hb_ready")
        yscale_ready = sem("yscale_ready")
        sum_read = sem("sum_read")
        hi_ready = sem("hi_ready")
        lo_ready = sem("lo_ready")
        result_out = [sem(f"result_out{u}") for u in range(2)]

        def wait(eng, s, value):
            if not (isinstance(value, int) and value <= 0):
                eng.wait_ge(s, value)

        def count(l, t):
            return l * NT + t + 1

        start_reg = {}

        def tile_of(eng, t):
            start = t * (P * NT * P)
            if not isinstance(t, int):
                if eng not in start_reg:
                    start_reg[eng] = eng.alloc_register("tile_start")
                eng.reg_mov(start_reg[eng], start)
                start = eng.snap(start_reg[eng])
            return scratch8[bass.ds(start, P * NT * P)].rearrange("(p f) -> p f", p=P)

        y_of = [ya, yb, ya, yb]

        block = ctx.enter_context(nc.Block())

        @block.sync
        def _(sp):
            def load_adj32(t, u, p):
                wait(sp, cast_done, t - 1)
                wait(sp, mask_done, 2 * (t - 1))
                sp.dma_start(adj32[:, u, :], adjT[t]).then_inc(adj32_in[u], 16)

            def load_xT(t, b):
                wait(sp, h_projected, t - 3)
                if isinstance(t, int) and t in (4, 5):
                    sp.wait_ge(sums_projected, t - 3)
                sp.dma_start(xT[:, b], x_cols[t]).then_inc(xT_in[b], 16)

            def store_a(t):
                sp.wait_ge(ab_ready, t + 1)
                sp.dma_start(a_rows[t].rearrange("(p a) -> p a", a=1), abcols[:, t, 0:1]).then_inc(
                    a_out_first if isinstance(t, int) and t < 2 else a_out, 16)

            def load_a(t, u):
                wait(sp, prod_ready, 2 * (t - 1))
                sp.dma_start(a_bc[:, u, :], a_rows[t].partition_broadcast(P)).then_inc(a_in[u], 16)

            sp.dma_start(wh[:], W_sa).then_inc(wh_in, 16)
            load_xT(0, 0)
            sp.dma_start(asa_bc[:], a_sa.partition_broadcast(P)).then_inc(asa_in, 16)
            load_xT(1, 1)
            sp.dma_start(wg[:, :, 0:D], W_gcnb).then_inc(wg_in, 16)
            sp.dma_start(wg[:, :, D:D + 4], gate_cols).then_inc(wg_in, 16)
            sp.dma_start(gate_bc[:], gate_bias.partition_broadcast(P)).then_inc(wg_in, 16)
            load_xT(2, 2)
            load_xT(3, 3)
            sp.dma_start(w2a_sb, W2a).then_inc(late_in, 16)
            sp.dma_start(w2b_sb, W2bT).then_inc(late_in, 16)
            sp.dma_start(b1col[:], b2a).then_inc(late_in, 16)
            sp.dma_start(bc_bc[:], b2b.partition_broadcast(P)).then_inc(late_in, 16)
            sp.dma_start(w1, W1g).then_inc(late_in, 16)
            sp.dma_start(w3, W3T).then_inc(late_in, 16)
            sp.dma_start(bg_bc[:], b_gcnb.partition_broadcast(P)).then_inc(late_in, 16)
            sp.dma_start(b1_bc[:], b1g.partition_broadcast(P)).then_inc(late_in, 16)
            sp.dma_start(b3_bc[:], b3.partition_broadcast(P)).then_inc(late_in, 16)

            def first(t, b):
                load_xT(t, b)
                store_a(t - 4)

            first(4, 0)
            first(5, 1)
            for q in range(2):
                for k in range(4):
                    first(6 + 4 * q + k, (6 + k) % 4)
                if q == 0:
                    sp.wait_ge(a_out_first, 16 * 2)
                    load_a(0, 0)
                    load_a(1, 1)
                else:
                    load_adj32(0, 0, 0)
            with sp.Fori(2, 5) as q:
                for k in range(4):
                    first(4 * q + 6 + k, (6 + k) % 4)
            load_adj32(1, 1, 0)
            sp.dma_start(xres[:], x_rows).then_inc(x_in, 16)
            for t in range(NT - 4, NT):
                store_a(t)
            sp.wait_ge(a_out, 16 * (NT - 2))

            def layer0(t, u, p, ahead=True):
                dst = tile_of(sp, t)
                sp.wait_ge(cast_done, t + 1)
                sp.dma_start(dst, adj8[:, u, :].bitcast(U8)).then_inc(adj8_out[u], 16)
                if ahead:
                    load_a(t + 2, u)
                    load_adj32(t + 2, u, p + 1)

            with sp.Fori(0, PAIRS - 1) as p:
                for u in range(2):
                    layer0(2 * p + u, u, p)
            for u in range(2):
                layer0(NT - 2 + u, u, PAIRS - 1, False)

            for u in range(2):
                sp.wait_ge(adj8_out[u], 16 * PAIRS)
            for l in range(1, 4):
                with sp.Fori(0, PAIRS) as p:
                    for u in range(2):
                        t = 2 * p + u
                        src = tile_of(sp, t)
                        sp.wait_ge(agg_done, count(l, t - 2))
                        sp.dma_start(adj8[:, u, :].bitcast(U8), src).then_inc(adj8_in[u], 16)

        @block.scalar
        def _(act):
            def first(t, u):
                act.wait_ge(small_ready, t + 1)
                nc.scalar.activation(ya[:, t, 0, 0:ONE], sum_ps[u][:, 0:ONE], ACT.Copy,
                                     scale=SY).then_inc(sums_hi, 1)
                nc.scalar.activation(abcols[:, t, :], small[:, u, 4:6], ACT.Exp,
                                     scale=-(1.0 - SLOPE))
                nc.scalar.activation(cols[:, t, 0:2], small[:, u, 4:6], ACT.Exp,
                                     scale=-SLOPE).then_inc(exps_ready, 1)
                act.wait_ge(ds_ready, t + 1)
                act.wait_ge(h_projected, t + 1)
                nc.scalar.activation(ym[:, t, 0, 0:D], att_ps[u][:, 0:D], ACT.Copy,
                                     scale=ds[:, u, :]).then_inc(h_hi, 1)

            def project_tiles(q0, q1):
                with act.Fori(q0, q1) as q:
                    for k in range(4):
                        first(4 * q + 2 + k, k % 2)

            def wait_for_cast(t, u, p):
                act.wait_ge(adj32_in[u], 16 * (p + 1))
                wait(act, agg_done, t - 1)
                wait(act, adj8_out[u], 16 * p)

            def cast(t, u):
                nc.scalar.copy(adj8[:, u, :], adj32[:, u, :], saturate=False).then_inc(cast_done, 1)

            def high_part(t, u, h):
                act.wait_ge(mask_done, 2 * t + h + 1)
                if h == 0:
                    wait(act, agg_done, t - 1)
                nc.scalar.copy(mhi[:, u, h * HALF * P:(h + 1) * HALF * P],
                               prod[:, h, :]).then_inc(mhi_ready, 1)

            def epilogue0(t, v):
                act.wait_ge(gate_in, t + 1)
                nc.scalar.activation(gates[:, v, :], gates[:, v, :], ACT.Sigmoid).then_inc(gate_out, 1)
                act.wait_ge(coef_ready, t + 1)
                nc.scalar.activation(t3[:], att_ps[v][:, 0:D], ACT.Copy,
                                     scale=coef[:, v, :]).then_inc(att_scaled, 1)
                act.wait_ge(z_ready, t + 1)
                nc.scalar.activation(sg[:], z[:], ACT.Sigmoid).then_inc(sig_ready, 1)

            def xT_high(l, t, v):
                act.wait_ge(transposed, count(l, t))
                nc.scalar.activation(xTh[:, v], tr_ps[:], ACT.Copy, scale=SX).then_inc(xT_hi, 1)

            def rows(l, t, v):
                act.wait_ge(projected, count(l, t))
                dst = y_of[l + 1][:, t, 0, 0:D]
                if l < 2:
                    act.wait_ge(yscale_ready, count(l, t))
                if l == 0:
                    nc.scalar.activation(dst, pj_ps[:, 0:D], ACT.Copy,
                                         scale=yscale[:, v, :]).then_inc(hi_ready, 1)
                elif l == 1:
                    act.wait_ge(hb_ready, t + 1)
                    nc.scalar.activation(dst, hb, ACT.Copy, scale=yscale[:, v, :]).then_inc(hi_ready, 1)
                else:
                    act.wait_ge(hb_ready, NT + t + 1)
                    nc.scalar.activation(dst, hb, ACT.Copy, scale=SY).then_inc(hi_ready, 1)

            def window0(t, u, p, ahead=True):
                v = 1 - u
                has_prev = not (isinstance(t, int) and t == 0)
                if ahead:
                    wait_for_cast(t + 1, v, p + u)
                if has_prev:
                    epilogue0(t - 1, v)
                if ahead:
                    high_part(t + 1, v, 0)
                    high_part(t + 1, v, 1)
                if has_prev:
                    xT_high(0, t - 1, v)
                if ahead:
                    cast(t + 1, v)
                if has_prev:
                    rows(0, t - 1, v)

            first(0, 0)
            first(1, 1)
            project_tiles(0, WEIGHTS_TURN)
            for k in range(4):
                first(4 * WEIGHTS_TURN + 2 + k, k % 2)
                if k < 2:
                    w, n = ((w1, 0), (w3, 2))[k]
                    act.wait_ge(late_in, 16 * 9)
                    nc.scalar.activation(w16[:, n, :, 0, :], w, ACT.Copy, scale=SW).then_inc(w16_hi, 1)
            for k in range(4):
                first(4 * COMB_TURN + 2 + k, k % 2)
                if k < KC:
                    act.wait_ge(comb_done, 1)
                    nc.scalar.activation(w16[:, 1, k, 0, :], comb_ps[k], ACT.Copy,
                                         scale=SW).then_inc(w16_hi, 1)
            project_tiles(COMB_TURN + 1, TURNS)

            high_part(0, 0, 0)
            high_part(0, 0, 1)
            for u in range(2):
                window0(u, u, 0)
            with act.Fori(1, PAIRS - 1) as p:
                for u in range(2):
                    window0(2 * p + u, u, p)
            for u in range(2):
                window0(NT - 2 + u, u, PAIRS - 1, ahead=(u == 0))

            epilogue0(NT - 1, 1)
            xT_high(0, NT - 1, 1)
            rows(0, NT - 1, 1)
            for l in range(1, 3):
                xT_high(l, 0, 0)
                with act.Fori(0, PAIRS - 1) as p:
                    for v in range(2):
                        rows(l, 2 * p + v, v)
                        xT_high(l, 2 * p + 1 + v, 1 - v)
                for v in range(2):
                    rows(l, NT - 2 + v, v)
                    if v == 0:
                        xT_high(l, NT - 1, 1)
            with act.Fori(0, PAIRS) as p:
                for v in range(2):
                    act.wait_ge(x_ready, count(3, 2 * p + v))
                    act.dma_start(out[2 * p + v], xn[:, v, :]).then_inc(result_out[v], 16)
            for v in range(2):
                act.wait_ge(result_out[v], 16 * PAIRS)

        @block.gpsimd
        def _(pool):
            nc.gpsimd.memset(minus_half[:], -0.5).then_inc(consts_made, 1)
            nc.gpsimd.memset(ident[:], 0.0).then_inc(ident_made, 1)
            pool.wait_ge(ident_made, 1)
            nc.gpsimd.affine_select(out=ident[:], in_=ident[:], compare_op=ALU.not_equal, fill=1.0, base=0,
                                    pattern=[[-1, P]], channel_multiplier=1).then_inc(ident_made, 1)
            pool.wait_ge(ident_made, 2)
            nc.gpsimd.tensor_copy(ident16[:], ident[:]).then_inc(ident_made, 1)
            nc.gpsimd.memset(ya[:, :, 0, ONE:ONE + 1], 1.0).then_inc(ident_made, 1)
            pool.wait_ge(consts_made, 1)

            def product(t, u, h, p):
                if h == 0:
                    pool.wait_ge(a_in[u], 16 * (p + 1))
                wait(pool, mlo_ready, 2 * (t - 1) + h + 1)
                wait(pool, mhi_ready, 2 * (t - 1) + h + 1)
                b = abcols[:, h * HALF:(h + 1) * HALF, 1:2].broadcast_to([P, HALF, P])
                a = a_bc[:, u:u + 1, :].broadcast_to([P, HALF, P])
                nc.gpsimd.tensor_tensor(prod[:, h, :].rearrange("p (j i) -> p j i", i=P), a, b,
                                        ALU.mult).then_inc(prod_ready, 1)

            def power(l, t, v):
                n = 3 if l == 0 else 1
                pool.wait_ge(var_ready, count(l, t))
                nc.gpsimd.tensor_tensor(pow_out[:, v, 0:n], pow_in[:, v, 0:n], minus_half[:, 0:n],
                                        ALU.pow).then_inc(pow_ready, 1)

            def save_x(l, t, v):
                pool.wait_ge(x_ready, count(l, t))
                nc.gpsimd.tensor_copy(xres[:, t, :], xn[:, v, :]).then_inc(x_saved, 1)

            def window0(t, u, p, ahead=True):
                v = 1 - u
                has_prev = not (isinstance(t, int) and t == 0)
                if has_prev:
                    power(0, t - 1, v)
                if ahead:
                    product(t + 2, u, 0, p + 1)
                if has_prev:
                    save_x(0, t - 1, v)
                if ahead:
                    product(t + 2, u, 1, p + 1)

            pool.wait_ge(ab_ready, HALF)
            product(0, 0, 0, 0)
            pool.wait_ge(adj32_in[0], 16)
            nc.gpsimd.tensor_copy(adj8[:, 0, :], adj32[:, 0, :], saturate=False).then_inc(cast_done, 1)
            pool.wait_ge(ab_ready, NT)
            product(0, 0, 1, 0)
            for h in range(2):
                product(1, 1, h, 0)
            for u in range(2):
                window0(u, u, 0)
            with pool.Fori(1, PAIRS - 1) as p:
                for u in range(2):
                    window0(2 * p + u, u, p)
            for u in range(2):
                window0(NT - 2 + u, u, PAIRS - 1, False)
            power(0, NT - 1, 1)
            save_x(0, NT - 1, 1)
            for l in range(1, 4):
                with pool.Fori(0, PAIRS) as p:
                    for v in range(2):
                        power(l, 2 * p + v, v)
                        if l < 3:
                            save_x(l, 2 * p + v, v)

        @block.vector
        def _(dve):
            done = [0]

            def link(ins):
                done[0] = done[0] + 1
                ins.then_inc(vec, 1)

            def linked():
                dve.wait_ge(vec, done[0])

            dve.wait_ge(wh_in, 16)
            dve.wait_ge(asa_in, 16)
            for c in range(KC):
                for side in range(2):
                    nc.vector.tensor_tensor_reduce(
                        out=(t1, t3, z, sg)[2 * c + side][:], in0=wh[:, c, :], in1=asa_bc[:, side, :], scale=1.0, scalar=0.0,
                        op0=ALU.mult, op1=ALU.add,
                        accum_out=wg[:, c, D + 4 + side:D + 5 + side]).then_inc(proj_cols_made, 1)

            def h_low(t, u):
                dve.wait_ge(h_hi, t + 1)
                nc.vector.scalar_tensor_tensor(ym[:, t, 1, 0:D], att_ps[u][:, 0:D], ds[:, u, :], ym[:, t, 0, 0:D],
                                               ALU.mult, ALU.subtract).then_inc(h_lo, 1)

            def rest(t, u):
                done[0] = t
                dve.wait_ge(ds_ready, t + 1)
                nc.vector.tensor_tensor(cols[:, t, 2:4], small[:, u, 2:4], gate_bc[:], ALU.add)
                link(nc.vector.tensor_copy(ym[:, t, 0, D:WM], ds[:, u, :]))
                h_low(t, u)
                linked()
                nc.vector.tensor_tensor(ym[:, t, 1, D:WM], ds[:, u, :], ym[:, t, 0, D:WM], ALU.subtract)

            def first(t, u):
                dve.wait_ge(sums_projected, t + 1)
                nc.vector.tensor_copy(small[:, u, :], sum_ps[u][:, D:WG]).then_inc(small_ready, 1)
                if not (isinstance(t, int) and t == 0):
                    rest(t - 1, 1 - u)
                dve.wait_ge(sums_hi, t + 1)
                nc.vector.scalar_tensor_tensor(ya[:, t, 1, 0:ONE], sum_ps[u][:, 0:ONE], SY, ya[:, t, 0, 0:ONE],
                                               ALU.mult, ALU.subtract).then_inc(sums_lo, 1)
                dve.wait_ge(exps_ready, t + 1)
                nc.vector.tensor_scalar(ds[:, u, :], cols[:, t, 1:2], SY, None, ALU.mult).then_inc(ds_ready, 1)
                nc.vector.tensor_scalar(abcols[:, t, :], abcols[:, t, :], SAB, None, ALU.mult).then_inc(ab_ready, 1)

            def project_tiles(q0, q1):
                with dve.Fori(q0, q1) as q:
                    for k in range(4):
                        first(4 * q + 2 + k, k % 2)

            def mask_quarter(k):
                if k == 0:
                    dve.wait_ge(prod_ready, 1)
                    dve.wait_ge(adj32_in[0], 16)
                part = slice(k * HALF * P // 4, (k + 1) * HALF * P // 4)
                quarter = nc.vector.scalar_tensor_tensor(prod[:, 0, part], prod[:, 0, part], SM, adj32[:, 0, part],
                                                         ALU.min, ALU.mult)
                if k == 3:
                    quarter.then_inc(mask_done, 1)

            def weight_low(n, c, w):
                nc.vector.scalar_tensor_tensor(w16[:, n, c, 1, :], w, SW, w16[:, n, c, 0, :],
                                               ALU.mult, ALU.subtract).then_inc(w16_ready, 1)

            dve.wait_ge(wg_in, 16 * 3)
            for u in range(2):
                first(u, u)
            project_tiles(0, WEIGHTS_TURN)
            for k in range(4):
                first(4 * WEIGHTS_TURN + 2 + k, k % 2)
                if k == 0:
                    dve.wait_ge(late_in, 16 * 9)
                    nc.vector.memset(b1rep[:], 1.0).then_inc(ones_made, 1)
                    dve.wait_ge(ones_made, 1)
                    nc.vector.tensor_scalar(b1rep[:], b1rep[:], b1col[:], None, ALU.mult).then_inc(comb_ready, 1)
                else:
                    dve.wait_ge(w16_hi, 1 + k // 3)
                    weight_low(*((0, 0, w1[:, 0, :]), (0, 1, w1[:, 1, :]), (2, 0, w3[:, 0, :]))[k - 1])
            for k in range(4):
                first(4 * COMB_TURN + 2 + k, k % 2)
                if k == 0:
                    dve.wait_ge(comb_done, 1)
                    nc.vector.tensor_tensor(bc_bc[:], b1w2_ps, bc_bc[:], ALU.add).then_inc(comb_saved, 1)
                elif k <= KC:
                    dve.wait_ge(w16_hi, 2 + k)
                    weight_low(1, k - 1, comb_ps[k - 1])
                else:
                    weight_low(2, 1, w3[:, 1, :])
            project_tiles(COMB_TURN + 1, MASK_TURN)
            for k in range(4):
                first(4 * MASK_TURN + 2 + k, k % 2)
                mask_quarter(k)
            project_tiles(MASK_TURN + 1, TURNS)
            rest(NT - 1, 1)
            base0 = NT

            def mask(t, u, h, p):
                dve.wait_ge(prod_ready, 2 * t + h + 1)
                if h == 0:
                    dve.wait_ge(adj32_in[u], 16 * (p + 1))
                nc.vector.scalar_tensor_tensor(prod[:, h, :], prod[:, h, :], SM,
                                               adj32[:, u, h * HALF * P:(h + 1) * HALF * P],
                                               ALU.min, ALU.mult).then_inc(mask_done, 1)

            def low_part(t, u, h):
                part = slice(h * HALF * P, (h + 1) * HALF * P)
                dve.wait_ge(mhi_ready, 2 * t + h + 1)
                nc.vector.tensor_tensor(mlo[:, u, part], prod[:, h, :], mhi[:, u, part],
                                        ALU.subtract).then_inc(mlo_ready, 1)

            def variance(v):
                link(nc.vector.bn_stats(stats[:, 0:6], xs[:, v, :]))
                linked()
                nc.vector.tensor_copy(stats[:, 6:7], stats[:, 0:1])
                link(nc.vector.bn_aggr(mean_var[:, v, :], stats[:, 0:6]))
                linked()
                nc.vector.tensor_scalar(pow_in[:, v, 0:1], mean_var[:, v, 1:2], EPS_LN, None,
                                        ALU.add).then_inc(var_ready, 1)

            def normalize(l, t, v):
                dve.wait_ge(pow_ready, count(l, t))
                if l in (1, 2):
                    wait(dve, transposed, count(l, t - 2))
                    wait(dve, x_saved, count(l, t - 2))
                nc.vector.tensor_scalar(xn[:, v, :], xs[:, v, :], mean_var[:, v, 0:1], pow_out[:, v, 0:1],
                                        ALU.subtract, ALU.mult).then_inc(x_ready, 1)

            LINKS0 = 8

            def epilogue0(t, v, p, ahead):
                done[0] = base0 + LINKS0 * t
                T, M = sum_ps[v], att_ps[v]
                link(nc.vector.tensor_copy(own[:, v, 0:4], cols[:, t, 0:4]))
                dve.wait_ge(agg_done, t + 1)
                linked()
                nc.vector.scalar_tensor_tensor(gates[:, v, :], T[:, GA:GA + 2], 1.0 / SY, own[:, v, 2:4],
                                               ALU.mult, ALU.add).then_inc(gate_in, 1)
                link(nc.vector.tensor_scalar(den[:, 0:1], M[:, D:WM], own[:, v, 0:1], EPS_ATT * SM * SY,
                                             ALU.mult, ALU.add))
                linked()
                link(nc.vector.reciprocal(den[:, 1:2], den[:, 0:1]))
                link(nc.vector.scalar_tensor_tensor(t1[:], T[:, 0:D], 1.0 / SY, bg_bc[:], ALU.mult, ALU.add))
                dve.wait_ge(gate_out, t + 1)
                linked()
                nc.vector.scalar_tensor_tensor(coef[:, v, :], den[:, 1:2], own[:, v, 0:1], gates[:, v, 0:1],
                                               ALU.mult, ALU.mult).then_inc(coef_ready, 1)
                nc.vector.tensor_scalar(pow_in[:, v, 1:2], T[:, ONE:WT], TINY, None, ALU.max)
                nc.vector.tensor_scalar(pow_in[:, v, 2:3], T[:, ONE:WT], 1.0, TINY, ALU.add, ALU.max)
                link(nc.vector.tensor_scalar(den[:, 2:3], T[:, ONE:WT], 0.0, None, ALU.is_gt))
                if ahead:
                    mask(t + 2, v, 0, p)
                dve.wait_ge(att_scaled, t + 1)
                nc.vector.scalar_tensor_tensor(z[:], t1[:], gates[:, v, 1:2], t3[:],
                                               ALU.mult, ALU.add).then_inc(z_ready, 1)
                if ahead:
                    mask(t + 2, v, 1, p)
                dve.wait_ge(sig_ready, t + 1)
                if isinstance(t, int) and t == 0:
                    dve.wait_ge(x_in, 16)
                link(nc.vector.tensor_tensor(xs[:, v, :], sg[:], xres[:, t, :], ALU.add))
                linked()
                variance(v)
                if ahead:
                    low_part(t + 2, v, 0)
                normalize(0, t, v)
                nc.vector.tensor_tensor(cols[:, t, 4:5], pow_out[:, v, 1:2], den[:, 2:3], ALU.mult)
                nc.vector.tensor_copy(cols[:, t, 5:6], pow_out[:, v, 2:3])
                nc.vector.scalar_tensor_tensor(yscale[:, v, :], pow_out[:, v, 1:2], SY / (SX * SW), den[:, 2:3],
                                               ALU.mult, ALU.mult).then_inc(yscale_ready, 1)

            def xT_low(l, t, v):
                dve.wait_ge(xT_hi, count(l, t))
                nc.vector.scalar_tensor_tensor(xTl[:, v], tr_ps[:], SX, xTh[:, v],
                                               ALU.mult, ALU.subtract).then_inc(xT_ready, 1)

            def biased(l, t):
                dve.wait_ge(projected, count(l, t))
                nc.vector.scalar_tensor_tensor(hb, pj_ps[:, 0:D], 1.0 / (SX * SW), (bc_bc if l == 1 else b3_bc)[:],
                                               ALU.mult, ALU.add).then_inc(hb_ready, 1)

            def rows(l, t, v):
                y = y_of[l + 1]
                dve.wait_ge(projected, count(l, t))
                if l < 2:
                    dve.wait_ge(yscale_ready, count(l, t))
                if l == 0:
                    dve.wait_ge(hi_ready, count(l, t))
                    nc.vector.scalar_tensor_tensor(y[:, t, 1, 0:D], pj_ps[:, 0:D], yscale[:, v, :],
                                                   y[:, t, 0, 0:D], ALU.mult, ALU.subtract).then_inc(lo_ready, 1)
                else:
                    dve.wait_ge(hi_ready, count(l, t))
                    nc.vector.scalar_tensor_tensor(y[:, t, 1, 0:D], hb, yscale[:, v, :] if l == 1 else SY,
                                                   y[:, t, 0, 0:D], ALU.mult, ALU.subtract).then_inc(lo_ready, 1)

            LINKS, LINKS3 = 6, 4

            def epilogue(l, t, v):
                done[0] = base0 + LINKS0 * NT + LINKS * (NT * (l - 1) + t)
                A = sum_ps[v]
                link(nc.vector.tensor_copy(own[:, v, 4:6], cols[:, t, 4:6]))
                linked()
                if l == 1:
                    link(nc.vector.tensor_scalar(escale[:, v, :], own[:, v, 4:5], 1.0 / SY, None, ALU.mult))
                    nc.vector.tensor_scalar(yscale[:, v, :], own[:, v, 5:6], SY, None,
                                            ALU.mult).then_inc(yscale_ready, 1)
                else:
                    link(nc.vector.tensor_scalar(escale[:, v, :], own[:, v, 5:6], 1.0 / SY, None, ALU.mult))
                linked()
                dve.wait_ge(agg_done, count(l, t))
                wait(dve, x_saved, count(l - 1, t))
                if l == 1:
                    link(nc.vector.scalar_tensor_tensor(t1[:], A[:, D:2 * D], escale[:, v, :], b1_bc[:],
                                                        ALU.mult, ALU.add))
                    linked()
                    nc.vector.scalar_tensor_tensor(t3[:], A[:, 0:D], escale[:, v, :], t1[:],
                                                   ALU.mult, ALU.add).then_inc(sum_read, 1)
                    dve.wait_ge(sum_read, t + 1)
                    link(nc.vector.scalar_tensor_tensor(xs[:, v, :], t3[:], 0.0, xres[:, t, :], ALU.max, ALU.add))
                else:
                    link(nc.vector.scalar_tensor_tensor(t1[:], A[:, D:2 * D], escale[:, v, :], xres[:, t, :],
                                                        ALU.mult, ALU.add))
                    linked()
                    link(nc.vector.scalar_tensor_tensor(xs[:, v, :], A[:, 0:D], escale[:, v, :], t1[:],
                                                        ALU.mult, ALU.add))
                linked()
                variance(v)
                normalize(l, t, v)

            def epilogue3(t, v, p):
                done[0] = base0 + LINKS0 * NT + LINKS * NT * 2 + LINKS3 * t
                dve.wait_ge(agg_done, count(3, t))
                dve.wait_ge(x_ready, count(3, t - 2))
                dve.wait_ge(x_saved, count(2, t))
                link(nc.vector.scalar_tensor_tensor(t1[:], sum_ps[v][:, D:2 * D], 1.0 / SY, xres[:, t, :],
                                                    ALU.mult, ALU.add))
                linked()
                link(nc.vector.scalar_tensor_tensor(xs[:, v, :], sum_ps[v][:, 0:D], 1.0 / SY, t1[:],
                                                    ALU.mult, ALU.add))
                linked()
                wait(dve, result_out[v], 16 * p)
                if isinstance(t, int):
                    dve.wait_ge(transposed, count(2, NT - 1))
                    dve.wait_ge(x_saved, count(2, NT - 1))
                variance(v)
                normalize(3, t, v)

            def window0(t, u, p, ahead=True):
                v = 1 - u
                has_prev = not (isinstance(t, int) and t == 0)
                if has_prev:
                    epilogue0(t - 1, v, p + u, ahead)
                else:
                    for h in range(2):
                        mask(1, 1, h, 0)
                    low_part(1, 1, 0)
                if ahead:
                    low_part(t + 1, v, 1)
                if has_prev:
                    xT_low(0, t - 1, v)
                    rows(0, t - 1, v)

            low_part(0, 0, 0)
            mask(0, 0, 1, 0)
            low_part(0, 0, 1)
            for u in range(2):
                window0(u, u, 0)
            with dve.Fori(1, PAIRS - 1) as p:
                for u in range(2):
                    window0(2 * p + u, u, p)
            for u in range(2):
                window0(NT - 2 + u, u, PAIRS - 1, ahead=(u == 0))
            epilogue0(NT - 1, 1, PAIRS, False)
            xT_low(0, NT - 1, 1)
            rows(0, NT - 1, 1)

            def turn(l, p, first=False):
                for v in range(2):
                    t = 2 * p + v
                    if l < 3:
                        epilogue(l, t, v)
                        if not (first and v == 0):
                            biased(l, t - 1)
                            rows(l, t - 1, 1 - v)
                        xT_low(l, t, v)
                    else:
                        epilogue3(t, v, p)

            for l in range(1, 4):
                turn(l, 0, True)
                with dve.Fori(1, PAIRS) as p:
                    turn(l, p)
                if l < 3:
                    biased(l, NT - 1)
                    rows(l, NT - 1, 1)

        @block.tensor
        def _(pe):
            def project_sums(t, u, b):
                wait(pe, sums_lo, t - 1)
                for c in range(KC):
                    last = nc.tensor.matmul(sum_ps[u][:, 0:WG], xT[:, b, c, :], wg[:, c, :],
                                            start=(c == 0), stop=(c == KC - 1))
                last.then_inc(sums_projected, 1)

            def project_h(t, u, b):
                wait(pe, h_lo, t - 1)
                for c in range(KC):
                    last = nc.tensor.matmul(att_ps[u][:, 0:D], xT[:, b, c, :], wh[:, c, :],
                                            start=(c == 0), stop=(c == KC - 1))
                last.then_inc(h_projected, 1)

            def project_tiles(q0, q1):
                with pe.Fori(q0, q1) as q:
                    for k in range(4):
                        t, b = 4 * q + 2 + k, (2 + k) % 4
                        pe.wait_ge(xT_in[b], 16 * (q + (2 + k) // 4 + 1))
                        project_sums(t, k % 2, b)
                        project_h(t, k % 2, b)

            pe.wait_ge(wh_in, 16)
            for t in range(2):
                pe.wait_ge(xT_in[t], 16)
                project_h(t, t, t)
            pe.wait_ge(wg_in, 16 * 3)
            pe.wait_ge(proj_cols_made, 2 * KC)
            for t in range(2):
                project_sums(t, t, t)
            project_tiles(0, WEIGHTS_TURN + 1)

            pe.wait_ge(comb_ready, 1)
            pe.wait_ge(late_in, 16 * 9)
            for c in range(KC):
                nc.tensor.matmul(comb_ps[c], w2a_sb[:, c * P:(c + 1) * P], w2b_sb, start=True, stop=True)
            nc.tensor.matmul(b1w2_ps, b1rep[:], w2b_sb, start=True, stop=True).then_inc(comb_done, 1)
            project_tiles(WEIGHTS_TURN + 1, TURNS)

            pe.wait_ge(sums_lo, NT)
            pe.wait_ge(comb_saved, 1)
            pe.wait_ge(w16_ready, 3 * KC)
            pe.wait_ge(ident_made, 4)

            def transpose(l, t, v):
                pe.wait_ge(x_ready, count(l, t))
                wait(pe, xT_ready, count(l, t) - 1)
                for c in range(KC):
                    last = nc.tensor.transpose(tr_ps[:, c, :], xn[:, v, c * P:(c + 1) * P], ident[:])
                last.then_inc(transposed, 1)

            def project(l, t, v):
                pe.wait_ge(xT_ready, count(l, t))
                wait(pe, lo_ready, count(l, t) - 1)
                terms = [(x, c, part) for c in range(KC) for x, part in ((xTh, 0), (xTh, 1), (xTl, 0))]
                for n, (x, c, part) in enumerate(terms):
                    last = nc.tensor.matmul(pj_ps[:, 0:D], x[:, v, c, :], w16[:, l, c, part, :],
                                            start=(n == 0), stop=(n == len(terms) - 1))
                last.then_inc(projected, 1)

            def window0(t, u):
                v = 1 - u
                has_prev = not (isinstance(t, int) and t == 0)
                second = isinstance(t, int) and t == 1
                wait(pe, x_ready, t - 1)

                def attention(last_part):
                    for j in range(NT):
                        if j % HALF == 0:
                            pe.wait_ge(mlo_ready, 2 * t + j // HALF + 1)
                        if not last_part and j == NT - 1:
                            pe.wait_ge(cast_done, t + 1)
                        hi, lo = mhi[:, u, j * P:(j + 1) * P], mlo[:, u, j * P:(j + 1) * P]
                        nc.tensor.matmul(att_ps[u][:, 0:WM], hi, ym[:, j, 0, 0:WM], start=(j == 0), stop=False)
                        nc.tensor.matmul(att_ps[u][:, 0:WM], hi, ym[:, j, 1, 0:WM], start=False, stop=False)
                        last = nc.tensor.matmul(att_ps[u][:, 0:WM], lo, ym[:, j, 0, 0:WM],
                                                start=False, stop=(j == NT - 1))
                    if last_part:
                        last.then_inc(agg_done, 1)

                def neighbours(last_part):
                    for j in range(NT):
                        if has_prev and j == (SECOND_TRANSPOSE_AT if second else TRANSPOSE0_AT):
                            transpose(0, t - 1, v)
                        if has_prev and j == (SECOND_PROJECT_AT if second else PROJECT0_AT):
                            project(0, t - 1, v)
                        w = adj8[:, u, j * P:(j + 1) * P]
                        nc.tensor.matmul(sum_ps[u][:, 0:WT], w, ya[:, j, 0, 0:WT], start=(j == 0), stop=False)
                        last = nc.tensor.matmul(sum_ps[u][:, 0:ONE], w, ya[:, j, 1, 0:ONE], start=False,
                                                stop=(j == NT - 1))
                    if last_part:
                        last.then_inc(agg_done, 1)

                if has_prev:
                    attention(False)
                    neighbours(True)
                else:
                    pe.wait_ge(cast_done, 1)
                    neighbours(False)
                    attention(True)

            for u in range(2):
                window0(u, u)
            with pe.Fori(1, PAIRS) as p:
                for u in range(2):
                    window0(2 * p + u, u)

            def opening(l, t, u, p):
                pe.wait_ge(x_ready, count(l, t - 2))
                pe.wait_ge(adj8_in[u], 16 * (PAIRS * (l - 1) + p + 1))
                if l == 2:
                    nc.tensor.matmul(sum_ps[u][:], ident16[:], y_of[l][:, t, :, 0:D], start=True, stop=False)
                else:
                    nc.tensor.matmul(idle_ps[:, 0:1], ident16[:], ident16[:, 0:1], start=True, stop=True)

            def source(l, u, j):
                ins = nc.tensor.matmul(sum_ps[u][:], adj8[:, u, j * P:(j + 1) * P], y_of[l][:, j, :, 0:D],
                                       start=(l != 2 and j == 0), stop=(j == NT - 1))
                if j == NT - 1:
                    ins.then_inc(agg_done, 1)

            def start(l):
                if l == 2:
                    pe.wait_ge(lo_ready, count(1, 1))
                opening(l, 0, 0, 0)
                between = BETWEEN[l - 1]
                steps = ([(0, j) for j in range(NT - 1)] + [(1, j) for j in range(between)] + [(0, NT - 1)]
                         + [(1, j) for j in range(between, NT)])
                for n, (u, j) in enumerate(steps):
                    if n == PROJECT_AT and l > 1:
                        project(l - 1, NT - 2, 0)
                    if n == START_TRANSPOSE_AT[l - 1]:
                        transpose(l - 1, NT - 1, 1)
                    if n == START_PROJECT_AT[l - 1]:
                        project(l - 1, NT - 1, 1)
                    if (u, j) == (1, 0):
                        opening(l, 1, 1, 0)
                    if (u, j) == (1, NT - 1) and l < 3:
                        transpose(l, 0, 0)
                    if u == 0:
                        pe.wait_ge(lo_ready, count(l - 1, j))
                    source(l, u, j)

            def window(l, t, u, p):
                opening(l, t, u, p)
                for j in range(NT):
                    if l < 3:
                        if j == PROJECT_AT:
                            project(l, t - 2, u)
                        if j == TRANSPOSE_AT:
                            transpose(l, t - 1, 1 - u)
                    source(l, u, j)

            for l in range(1, 4):
                start(l)
                with pe.Fori(1, PAIRS) as p:
                    for u in range(2):
                        window(l, 2 * p + u, u, p)


def kernel(**inputs):
    import numpy as np
    import concourse.bacc as bacc
    from concourse.bass_utils import run_bass_kernel_spmd as run

    v = {k: np.ascontiguousarray(a) for k, a in inputs.items()}
    pad = NT * P - N

    adjT = np.pad(v["adj"], ((0, pad), (0, pad))).reshape(NT, P, NT, P)
    xp = np.pad(v["x"], ((0, pad), (0, 0))).reshape(NT, P, D)
    chunks = lambda w: w.reshape(KC, P, -1).transpose(1, 0, 2)
    wa, wb = v["L0_gnn_Wa"].reshape(2, D), v["L0_gnn_Wb"].reshape(2, D)
    arrays = {
        "adjT": adjT.transpose(0, 3, 2, 1).reshape(NT, P, NT * P),
        "x_rows": xp.transpose(1, 0, 2),
        "x_cols": xp.reshape(NT, P, KC, P).transpose(0, 3, 2, 1),
        "W_sa": chunks(v["L0_gnn_W_sa"]),
        "a_sa": v["L0_gnn_a_sa"].reshape(2, D),
        "W_gcnb": chunks(v["L0_gnn_W_gcnb"]),
        "b_gcnb": v["L0_gnn_b_gcnb"],
        "gate_cols": chunks(np.stack([wa[0], wb[0], wa[1], wb[1]], axis=1)),
        "gate_bias": np.concatenate([v["L0_gnn_ba"], v["L0_gnn_bb"]]),
        "W1g": chunks(v["L1_gnn_W"]),
        "b1g": v["L1_gnn_b"],
        "W2a": v["L2_gnn_W1"],
        "b2a": v["L2_gnn_b1"].reshape(P, 1),
        "W2bT": v["L2_gnn_W2"].T,
        "b2b": v["L2_gnn_b2"],
        "W3T": chunks(v["L3_gnn_W"].T),
        "b3": v["L3_gnn_b"],
    }
    nc = bacc.Bacc("TRN2", target_bir_lowering=False, num_devices=1)
    arrays = {k: np.ascontiguousarray(a) for k, a in arrays.items()}
    aps = [nc.dram_tensor(k, a.shape, mybir.dt.from_np(a.dtype), kind="ExternalInput").ap()
           for k, a in arrays.items()]
    out = nc.dram_tensor("out", (NT, P, D), F32, kind="ExternalOutput").ap()
    resnorm_gnn_kernel(nc, *aps, out)
    r = run(nc, [arrays], core_ids=[0])
    return r.results[0]["out"].reshape(NT * P, D)[:N]
```
